# Optimizing a Trainium2 kernel written in Bass

```python
import numpy as np
import jax
import jax.numpy as jnp

def _softmax(x, axis=-1):
    return jax.nn.softmax(x, axis=axis)

def _gelu(x):
    return jax.nn.gelu(x, approximate=True)

def _silu(x):
    return jax.nn.silu(x)

def _sigmoid(x):
    return jax.nn.sigmoid(x)

def _layernorm(x, axis=-1, eps=1e-05):
    m = jnp.mean(x, axis=axis, keepdims=True)
    v = jnp.var(x, axis=axis, keepdims=True)
    return (x - m) / jnp.sqrt(v + eps)

def _scatter_add(tgt, idx, src, axis=0):
    return tgt.at[idx].add(src)

def _segment_sum(src, seg, n):
    return jax.ops.segment_sum(src, seg, n)
kernel_name = 'mk_dlrm_tower_d1_rec_r8_41bae5'

def setup_inputs(seed: int=0):
    np.random.seed(seed)
    _w = jnp.asarray

    def _rec_inputs():
        import jax
        import jax.numpy as jnp
        _tk = jax.random.key(seed)
        ids = jnp.stack([jax.random.randint(jax.random.fold_in(_tk, 200 + f), (2048,), 0, v, jnp.int32) for f, v in enumerate([125000, 12500, 1000, 12500, 12500, 1000, 12500, 1000, 1250, 1250, 1000, 1000, 1000, 1250, 1250, 1250, 12500, 12500, 12500, 12500, 1250, 1250, 1000, 1250, 1000, 1250])], axis=1)
        tbl_0 = 0.05 * jax.random.normal(jax.random.fold_in(_tk, 500 + 0), (125000, 128), jnp.float32)
        tbl_1 = 0.05 * jax.random.normal(jax.random.fold_in(_tk, 500 + 1), (12500, 128), jnp.float32)
        tbl_2 = 0.05 * jax.random.normal(jax.random.fold_in(_tk, 500 + 2), (1000, 128), jnp.float32)
        tbl_3 = 0.05 * jax.random.normal(jax.random.fold_in(_tk, 500 + 3), (12500, 128), jnp.float32)
        tbl_4 = 0.05 * jax.random.normal(jax.random.fold_in(_tk, 500 + 4), (12500, 128), jnp.float32)
        tbl_5 = 0.05 * jax.random.normal(jax.random.fold_in(_tk, 500 + 5), (1000, 128), jnp.float32)
        tbl_6 = 0.05 * jax.random.normal(jax.random.fold_in(_tk, 500 + 6), (12500, 128), jnp.float32)
        tbl_7 = 0.05 * jax.random.normal(jax.random.fold_in(_tk, 500 + 7), (1000, 128), jnp.float32)
        tbl_8 = 0.05 * jax.random.normal(jax.random.fold_in(_tk, 500 + 8), (1250, 128), jnp.float32)
        tbl_9 = 0.05 * jax.random.normal(jax.random.fold_in(_tk, 500 + 9), (1250, 128), jnp.float32)
        tbl_10 = 0.05 * jax.random.normal(jax.random.fold_in(_tk, 500 + 10), (1000, 128), jnp.float32)
        tbl_11 = 0.05 * jax.random.normal(jax.random.fold_in(_tk, 500 + 11), (1000, 128), jnp.float32)
        tbl_12 = 0.05 * jax.random.normal(jax.random.fold_in(_tk, 500 + 12), (1000, 128), jnp.float32)
        tbl_13 = 0.05 * jax.random.normal(jax.random.fold_in(_tk, 500 + 13), (1250, 128), jnp.float32)
        tbl_14 = 0.05 * jax.random.normal(jax.random.fold_in(_tk, 500 + 14), (1250, 128), jnp.float32)
        tbl_15 = 0.05 * jax.random.normal(jax.random.fold_in(_tk, 500 + 15), (1250, 128), jnp.float32)
        tbl_16 = 0.05 * jax.random.normal(jax.random.fold_in(_tk, 500 + 16), (12500, 128), jnp.float32)
        tbl_17 = 0.05 * jax.random.normal(jax.random.fold_in(_tk, 500 + 17), (12500, 128), jnp.float32)
        tbl_18 = 0.05 * jax.random.normal(jax.random.fold_in(_tk, 500 + 18), (12500, 128), jnp.float32)
        tbl_19 = 0.05 * jax.random.normal(jax.random.fold_in(_tk, 500 + 19), (12500, 128), jnp.float32)
        tbl_20 = 0.05 * jax.random.normal(jax.random.fold_in(_tk, 500 + 20), (1250, 128), jnp.float32)
        tbl_21 = 0.05 * jax.random.normal(jax.random.fold_in(_tk, 500 + 21), (1250, 128), jnp.float32)
        tbl_22 = 0.05 * jax.random.normal(jax.random.fold_in(_tk, 500 + 22), (1000, 128), jnp.float32)
        tbl_23 = 0.05 * jax.random.normal(jax.random.fold_in(_tk, 500 + 23), (1250, 128), jnp.float32)
        tbl_24 = 0.05 * jax.random.normal(jax.random.fold_in(_tk, 500 + 24), (1000, 128), jnp.float32)
        tbl_25 = 0.05 * jax.random.normal(jax.random.fold_in(_tk, 500 + 25), (1250, 128), jnp.float32)
        _rk = jax.random.fold_in(_tk, 7)
        r_dense_x = -0.000514642 + 1.00011 * jax.random.normal(jax.random.fold_in(_rk, 101), (2048, 128), jnp.float32)
        W_top1 = 0.0456912 * jax.random.normal(jax.random.fold_in(_tk, 801), (479, 512), jnp.float32)
        W_top2 = 0.0441942 * jax.random.normal(jax.random.fold_in(_tk, 802), (512, 256), jnp.float32)
        W_top3 = 0.0625 * jax.random.normal(jax.random.fold_in(_tk, 803), (256, 1), jnp.float32)
        b_top1 = jnp.zeros((512,), jnp.float32)
        b_top2 = jnp.zeros((256,), jnp.float32)
        return (r_dense_x, ids, tbl_0, tbl_1, tbl_2, tbl_3, tbl_4, tbl_5, tbl_6, tbl_7, tbl_8, tbl_9, tbl_10, tbl_11, tbl_12, tbl_13, tbl_14, tbl_15, tbl_16, tbl_17, tbl_18, tbl_19, tbl_20, tbl_21, tbl_22, tbl_23, tbl_24, tbl_25, W_top1, b_top1, W_top2, b_top2, W_top3)
    r_dense_x, ids, tbl_0, tbl_1, tbl_2, tbl_3, tbl_4, tbl_5, tbl_6, tbl_7, tbl_8, tbl_9, tbl_10, tbl_11, tbl_12, tbl_13, tbl_14, tbl_15, tbl_16, tbl_17, tbl_18, tbl_19, tbl_20, tbl_21, tbl_22, tbl_23, tbl_24, tbl_25, W_top1, b_top1, W_top2, b_top2, W_top3 = _rec_inputs()

    def _L0_rec_setup():
        import jax, jax.numpy as jnp
        import numpy as np
        F = 26
        D = 128
        B = 2048
        _TRIU_I, _TRIU_J = np.triu_indices(F + 1, k=1)
        _TRIU_I = jnp.asarray(_TRIU_I)
        _TRIU_J = jnp.asarray(_TRIU_J)
        key = jax.random.key(seed)
        k1, k2 = jax.random.split(key)
        sparse_x = jax.random.normal(k1, (B, F, D), dtype=jnp.float32)
        dense_x = jax.random.normal(k2, (B, D), dtype=jnp.float32)
        return {'sparse_x': sparse_x, 'dense_x': dense_x}
    _L0_rec_all = _L0_rec_setup()
    _L0_rec_in = {k: v for k, v in _L0_rec_all.items() if k in ()}
    del _L0_rec_all
    return {'r_dense_x': r_dense_x, 'ids': ids, 'tbl_0': tbl_0, 'tbl_1': tbl_1, 'tbl_2': tbl_2, 'tbl_3': tbl_3, 'tbl_4': tbl_4, 'tbl_5': tbl_5, 'tbl_6': tbl_6, 'tbl_7': tbl_7, 'tbl_8': tbl_8, 'tbl_9': tbl_9, 'tbl_10': tbl_10, 'tbl_11': tbl_11, 'tbl_12': tbl_12, 'tbl_13': tbl_13, 'tbl_14': tbl_14, 'tbl_15': tbl_15, 'tbl_16': tbl_16, 'tbl_17': tbl_17, 'tbl_18': tbl_18, 'tbl_19': tbl_19, 'tbl_20': tbl_20, 'tbl_21': tbl_21, 'tbl_22': tbl_22, 'tbl_23': tbl_23, 'tbl_24': tbl_24, 'tbl_25': tbl_25, 'W_top1': W_top1, 'b_top1': b_top1, 'W_top2': W_top2, 'b_top2': b_top2, 'W_top3': W_top3}

def reference(r_dense_x, ids, tbl_0, tbl_1, tbl_2, tbl_3, tbl_4, tbl_5, tbl_6, tbl_7, tbl_8, tbl_9, tbl_10, tbl_11, tbl_12, tbl_13, tbl_14, tbl_15, tbl_16, tbl_17, tbl_18, tbl_19, tbl_20, tbl_21, tbl_22, tbl_23, tbl_24, tbl_25, W_top1, b_top1, W_top2, b_top2, W_top3):
    import jax
    import jax.numpy as jnp

    def _L0_rec_ref(sparse_x, dense_x):
        import jax, jax.numpy as jnp
        import numpy as np
        F = 26
        D = 128
        B = 2048
        _TRIU_I, _TRIU_J = np.triu_indices(F + 1, k=1)
        _TRIU_I = jnp.asarray(_TRIU_I)
        _TRIU_J = jnp.asarray(_TRIU_J)
        combined = jnp.concatenate([sparse_x, dense_x[:, None, :]], axis=1)
        interact = jnp.einsum('bfd,bgd->bfg', combined, combined)
        return interact[:, _TRIU_I, _TRIU_J]
    e = jnp.stack([tbl_0[ids[:, 0]], tbl_1[ids[:, 1]], tbl_2[ids[:, 2]], tbl_3[ids[:, 3]], tbl_4[ids[:, 4]], tbl_5[ids[:, 5]], tbl_6[ids[:, 6]], tbl_7[ids[:, 7]], tbl_8[ids[:, 8]], tbl_9[ids[:, 9]], tbl_10[ids[:, 10]], tbl_11[ids[:, 11]], tbl_12[ids[:, 12]], tbl_13[ids[:, 13]], tbl_14[ids[:, 14]], tbl_15[ids[:, 15]], tbl_16[ids[:, 16]], tbl_17[ids[:, 17]], tbl_18[ids[:, 18]], tbl_19[ids[:, 19]], tbl_20[ids[:, 20]], tbl_21[ids[:, 21]], tbl_22[ids[:, 22]], tbl_23[ids[:, 23]], tbl_24[ids[:, 24]], tbl_25[ids[:, 25]]], axis=1)
    z = _L0_rec_ref(e, r_dense_x)
    z = z.reshape(z.shape[0], -1)
    h = jnp.concatenate([z, r_dense_x], axis=1)
    h = jnp.maximum(h @ W_top1 + b_top1, 0.0)
    h = jnp.maximum(h @ W_top2 + b_top2, 0.0)
    y = h @ W_top3
    return y

_drawn_inputs = setup_inputs


def setup_inputs(seed=0):
    import zlib

    import numpy as np

    out = dict(_drawn_inputs(seed))
    spreads = {'b_top1': (0.0, 0.1), 'b_top2': (0.0, 0.1)}
    factors = {}
    for name, (base, spread) in spreads.items():
        noise = np.random.default_rng([zlib.crc32(name.encode()), seed]).standard_normal(out[name].shape)
        drawn = base * np.exp(spread * noise) if base else spread * noise
        out[name] = jnp.asarray(drawn.astype(out[name].dtype))
    for name, factor in factors.items():
        out[name] = (out[name] * factor).astype(out[name].dtype)
    return out
```

```python
import numpy as np
import concourse.bass as bass
import concourse.mybir as mybir
from contextlib import ExitStack

F32 = mybir.dt.float32
F32R = mybir.dt.float32r
I32 = mybir.dt.int32
U32 = mybir.dt.uint32
ALU = mybir.AluOpType
ACT = mybir.ActivationFunctionType

BATCH, DIM = 2048, 128
N_TABLES = 26
N_FEAT = N_TABLES + 1
SELECTED = [2, 5, 7, 10, 11, 12]
GATHERED = [t for t in range(N_TABLES) if t not in SELECTED]
SEL_ROWS = 1000
N_SEL, N_GATH = len(SELECTED), len(GATHERED)
ORDER = GATHERED + [N_TABLES] + SELECTED
DENSE_AT = N_GATH

TILE = 128
CHUNK_TILES = 2
CHUNK = TILE * CHUNK_TILES
N_CHUNKS = BATCH // CHUNK

SPLIT = 8
SEL_K = SEL_ROWS // SPLIT
OH_RING = 2

BANK_FEATS = 4
N_TGRP = -(-(N_GATH + 1) // BANK_FEATS)
T_GROUPS = [list(range(BANK_FEATS * g, min(BANK_FEATS * (g + 1), N_GATH + 1))) for g in range(N_TGRP)]

HALF_FEAT = N_FEAT // 2
N_PAIRS = N_FEAT * HALF_FEAT
Z_COLS = N_FEAT + HALF_FEAT
PAIR_TILES = 3
F_PER_TILE = N_FEAT // PAIR_TILES
PAIR_K = F_PER_TILE * HALF_FEAT

QUAD = 4
GRAM_SAMPLES = 32
N_GGRP = TILE // GRAM_SAMPLES
GRAM_N = QUAD * N_FEAT
FEAT_PAD = 32

H1, H2 = 512, 256
M1, M2 = H1 // 128, H2 // 128
MLP_STEPS = M1 + M2 + 1


class Chunk:

    def __init__(self, number, half, parity, least):
        self.c = number
        self.half = half
        self.par = parity
        self.least = least

    def next(self):
        return Chunk(self.c + 1, self.half + self.par, 1 - self.par, self.least + 1)


def build(nc, ids_gath, ids_sel, x, tables, w1_pairs, w1_dense, b1, w2, b2, w3, out):
    ctx = ExitStack()
    with ctx:
        def sb(name, shape, dt=F32):
            return ctx.enter_context(nc.sbuf_tensor(name, shape, dt))

        def sem(name):
            return ctx.enter_context(nc.semaphore(name))

        ident = sb("ident", [128, 128])
        idx = [sb(f"idx{p}", [128, CHUNK_TILES, N_GATH], I32) for p in range(2)]
        ids_row = [sb(f"ids_row{p}", [128, N_SEL, CHUNK], I32) for p in range(2)]
        rows = [sb(f"rows{t}", [128, N_GATH, DIM]) for t in range(CHUNK_TILES)]
        xin = [sb(f"xin{t}", [128, DIM]) for t in range(CHUNK_TILES)]
        table_hi = [sb(f"table_hi{k}", [SEL_K, SPLIT * DIM], F32R) for k in range(N_SEL)]
        table_lo = [sb(f"table_lo{k}", [SEL_K, SPLIT * DIM], F32R) for k in range(N_SEL)]
        row_no_i = sb("row_no_i", [128, SPLIT], I32)
        row_no = sb("row_no", [128, SPLIT])
        onehot = [sb(f"onehot{k}", [128, SPLIT, CHUNK], F32R) for k in range(OH_RING)]
        xT = [sb(f"xT{p}", [128, CHUNK_TILES, TILE, FEAT_PAD]) for p in range(2)]
        denseT = [sb(f"denseT{p}", [128, CHUNK]) for p in range(2)]
        zsb = sb("zsb", [128, N_FEAT * TILE])
        table_raw = [zsb[0:SEL_K, k * SPLIT * DIM:(k + 1) * SPLIT * DIM] for k in range(2)]
        zpair = [sb(f"zpair{p}", [128, PAIR_TILES, CHUNK]) for p in range(2)]
        w1p_sb = sb("w1p_sb", [PAIR_K, PAIR_TILES, H1])
        w1d_sb = sb("w1d_sb", [128, H1])
        w2_sb = sb("w2_sb", [128, M1, H2])
        w3_sb = sb("w3_sb", [128, M2])
        b1_sb = sb("b1_sb", [128, M1])
        b2_sb = sb("b2_sb", [128, M2])
        h1 = sb("h1", [128, M1, CHUNK])
        h2 = sb("h2", [128, M2, CHUNK])
        y_sb = sb("y_sb", [1, CHUNK])

        ps_t = [ctx.enter_context(nc.psum_tensor(f"ps_t{k}", [128, BANK_FEATS, TILE], F32)) for k in range(2)]
        ps_g = [ctx.enter_context(nc.psum_tensor(f"ps_g{k}", [128, 2, 512], F32)) for k in range(2)]
        ps_s = ctx.enter_context(nc.psum_tensor("ps_s", [128, 512], F32))
        ps_m = ctx.enter_context(nc.psum_tensor("ps_m", [128, 512], F32))

        z_dram = [nc.dram_tensor(f"z_dram{t}", [N_FEAT, Z_COLS * TILE], F32, kind="Internal") for t in range(CHUNK_TILES)]

        s_zero = sem("s_zero")
        s_const = sem("s_const")
        s_rowno = sem("s_rowno")
        s_pad = sem("s_pad")
        s_raw = [sem(f"s_raw{k}") for k in range(N_SEL)]
        s_hi = sem("s_hi")
        s_lo = sem("s_lo")
        s_w = sem("s_w")
        s_idx = [sem(f"s_idx{p}") for p in range(2)]
        s_ids = [sem(f"s_ids{p}") for p in range(2)]
        s_x = [sem(f"s_x{t}") for t in range(CHUNK_TILES)]
        s_place = sem("s_place")
        s_rows = [[sem(f"s_rows{t}_{g}") for g in range(N_TGRP)] for t in range(CHUNK_TILES)]
        s_tr = sem("s_tr")
        s_tcopy = [sem(f"s_tcopy{k}") for k in range(2)]
        s_oh = sem("s_oh")
        s_sel = sem("s_sel")
        s_scopy = sem("s_scopy")
        s_gram = sem("s_gram")
        s_gcopy = [sem(f"s_gcopy{k}") for k in range(2)]
        s_zw = [sem(f"s_zw{t}") for t in range(CHUNK_TILES)]
        s_zr = [sem(f"s_zr{t}") for t in range(CHUNK_TILES)]
        s_mlp = sem("s_mlp")
        s_mcopy = sem("s_mcopy")
        s_y = sem("s_y")

        block = ctx.enter_context(nc.Block())

        def chunks(eng, body):
            body(Chunk(0, 0, 0, 0))
            with eng.Fori(0, (N_CHUNKS - 2) // 2) as i:
                first = Chunk(i * 2 + 1, i, 1, 1)
                body(first)
                body(first.next())
            body(Chunk(N_CHUNKS - 1, (N_CHUNKS - 1) // 2, (N_CHUNKS - 1) % 2, N_CHUNKS - 1))

        def middle_steps(ch, t):
            sel = list(range(N_SEL)) if ch.least < N_CHUNKS - 1 else []
            mlp = list(range(MLP_STEPS)) if ch.least > 0 else []
            cut_s, cut_m = -(-len(sel) // 2), 3
            sel, mlp = (sel[:cut_s], mlp[:cut_m]) if t == 0 else (sel[cut_s:], mlp[cut_m:])
            steps = []
            if t == 0 and sel:
                steps.append(("sel", sel.pop(0)))
            while sel or mlp:
                if t == 0:
                    order = (sel, "sel"), (mlp, "mlp")
                else:
                    order = (mlp, "mlp"), (sel, "sel")
                for left, kind in order:
                    if left:
                        steps.append((kind, left.pop(0)))
            return steps

        def copier(t, g):
            return (t * N_TGRP + g) % 2

        def bank_use(ch, t, g):
            return ch.c * N_TGRP + (t * N_TGRP + g) // 2

        def tgroups(ch, t, g):
            return (ch.c * CHUNK_TILES + t) * N_TGRP + g

        def grams(ch, t, u):
            return (ch.c * CHUNK_TILES + t) * N_GGRP + u

        @block.sync
        def _(sp):
            def load_idx(first_tile, par):
                sp.dma_start(idx[par][:, :, :], ids_gath[bass.ds(first_tile, CHUNK_TILES), :, :]
                             .rearrange("t p f -> p t f")).then_inc(s_idx[par], 16)

            def load_ids(sample, par):
                sp.dma_start(ids_row[par][:, :, :],
                             ids_sel[:, bass.ds(sample, CHUNK)].partition_broadcast(128)).then_inc(s_ids[par], 16)

            def load_x(sample, t):
                sp.dma_start(xin[t][:, :], x[bass.ds(sample, TILE), :]).then_inc(s_x[t], 16)

            sp.sem_inc(s_y, 16)
            load_idx(0, 0)
            load_ids(0, 0)
            for k in range(2):
                sp.dma_start(table_raw[k], tables[SELECTED[k]].rearrange("(p a) d -> p (a d)", a=SPLIT))\
                  .then_inc(s_raw[k], 16)
            load_idx(CHUNK_TILES, 1)
            for t in range(CHUNK_TILES):
                load_x(t * TILE, t)
            load_ids(CHUNK, 1)
            for k in range(2, N_SEL):
                sp.wait_ge(s_lo, k - 1)
                sp.dma_start(table_raw[k % 2], tables[SELECTED[k]].rearrange("(p a) d -> p (a d)", a=SPLIT))\
                  .then_inc(s_raw[k], 16)
            for dst, src in ((w1p_sb[:, :, :], w1_pairs.rearrange("(k p) n -> p k n", p=PAIR_K)),
                             (w1d_sb[:, :], w1_dense), (w2_sb[:, :, :], w2.rearrange("(k p) n -> p k n", p=128)),
                             (w3_sb[:, :], w3), (b1_sb[:, :], b1), (b2_sb[:, :], b2)):
                sp.dma_start(dst, src).then_inc(s_w, 16)

            def bounce(ch, t, copied, read, written, layer_done):
                sp.wait_ge(s_gcopy[0], copied)
                sp.wait_ge(s_gcopy[1], copied)
                if ch.least >= 1:
                    sp.wait_ge(s_zr[t], read)
                q = 32 * t
                sp.dma_start(z_dram[t][:, 0:N_FEAT * TILE], zsb[q:q + N_FEAT, :]).then_inc(s_zw[t], 16)
                sp.dma_start(z_dram[t][:, N_FEAT * TILE:Z_COLS * TILE], zsb[q:q + N_FEAT, 0:HALF_FEAT * TILE])\
                  .then_inc(s_zw[t], 16)
                sp.wait_ge(s_zw[t], written)
                if ch.least >= 1:
                    sp.wait_ge(s_mlp, layer_done)
                base = z_dram[t][:, :]
                for k in range(PAIR_TILES):
                    f0 = k * F_PER_TILE
                    diagonal = bass.AP(tensor=base.tensor, offset=(f0 * Z_COLS + f0 + 1) * TILE,
                                       ap=[[(Z_COLS + 1) * TILE, F_PER_TILE], [TILE, HALF_FEAT], [1, TILE]])
                    sp.dma_start(zpair[ch.par][0:PAIR_K, k, t * TILE:(t + 1) * TILE], diagonal)\
                      .then_inc(s_zr[t], 16)

            def store_y(copied, sample):
                sp.wait_ge(s_mcopy, copied)
                sp.dma_start(out[bass.ds(sample, CHUNK), :].rearrange("n o -> o n"), y_sb[:, :]).then_inc(s_y, 16)

            def held(value):
                if isinstance(value, int):
                    return value
                reg = sp.alloc_register(f"held{len(held_regs)}")
                held_regs.append(reg)
                sp.reg_mov(reg, value)
                return sp.snap(reg)

            held_regs = []

            def body(ch):
                not_last = ch.least < N_CHUNKS - 1
                if not_last:
                    x0, x1 = (ch.c + 1) * CHUNK, (ch.c + 1) * CHUNK + TILE
                    far_sample, far_tile = (ch.c + 2) % N_CHUNKS * CHUNK, (ch.c + 2) % N_CHUNKS * CHUNK_TILES
                if ch.least >= 1:
                    y0 = (ch.c - 1) * CHUNK
                ids_used = held(N_SEL * (ch.c + 1))
                transposed = [held(tgroups(ch, t + 1, 0)) for t in range(CHUNK_TILES)]
                y_copied = held(1 + MLP_STEPS * ch.c)
                counts = [held(16 * PAIR_TILES * ch.c), held(32 * (ch.c + 1)), held(1 + MLP_STEPS * (ch.c - 1))]
                copied = [held((ch.c * CHUNK_TILES + t + 1) * (N_GGRP // 2)) for t in range(CHUNK_TILES)]
                if not_last:
                    sp.wait_ge(s_oh, ids_used)
                    load_ids(far_sample, ch.par)
                    sp.wait_ge(s_tr, transposed[0])
                    load_x(x0, 0)
                bounce(ch, 0, copied[0], *counts)
                if not_last:
                    sp.wait_ge(s_tr, transposed[1])
                    load_x(x1, 1)
                    load_idx(far_tile, ch.par)
                if ch.least >= 1:
                    store_y(y_copied, y0)
                bounce(ch, 1, copied[1], *counts)

            chunks(sp, body)
            store_y(1 + MLP_STEPS * N_CHUNKS, BATCH - CHUNK)
            sp.wait_ge(s_y, 16 * (1 + N_CHUNKS))
            for p in range(2):
                sp.wait_ge(s_idx[p], 16 * (1 + (N_CHUNKS - p) // 2))
                sp.wait_ge(s_ids[p], 16 * (1 + (N_CHUNKS - p) // 2))

        @block.gpsimd
        def _(pool):
            def body(ch):
                pool.wait_ge(s_idx[ch.par], 16 * (ch.half + 1))
                for t in range(CHUNK_TILES):
                    for g, feats in enumerate(T_GROUPS):
                        if ch.least >= 1:
                            pool.wait_ge(s_tr, tgroups(ch, t, g) - CHUNK_TILES * N_TGRP + 1)
                            pool.sem_inc(s_place, 1)
                        for f in feats:
                            if f != DENSE_AT:
                                pool.indirect_dma_start(
                                    rows[t][:, f, :], None, tables[GATHERED[f]][:, :],
                                    bass.IndirectOffsetOnAxis(ap=idx[ch.par][:, t, f:f + 1].bitcast(U32), axis=0),
                                ).then_inc(s_rows[t][g], 16)
                    if t == 0 and ch.least == 0:
                        pool.memset(ident[:, :], 0.0).then_inc(s_zero, 1)
                        pool.iota(row_no_i[:, :], pattern=[[1, SPLIT]], base=0, channel_multiplier=SPLIT)\
                            .then_inc(s_const, 1)
                        pool.wait_ge(s_zero, 1)
                        pool.affine_select(out=ident[:, :], in_=ident[:, :], compare_op=ALU.not_equal, fill=1.0,
                                           base=0, pattern=[[-1, 128]], channel_multiplier=1).then_inc(s_const, 1)

            chunks(pool, body)

        @block.tensor
        def _(pe):
            def transposes(ch, t):
                for g, feats in enumerate(T_GROUPS):
                    n_rows = len([f for f in feats if f != DENSE_AT])
                    if n_rows:
                        pe.wait_ge(s_rows[t][g], 16 * n_rows * (ch.c + 1))
                    if DENSE_AT in feats:
                        pe.wait_ge(s_x[t], 16 * (ch.c + 1))
                    k = copier(t, g)
                    if ch.least >= 1 or (t * N_TGRP + g) // 2 >= 1:
                        pe.wait_ge(s_tcopy[k], bank_use(ch, t, g))
                    for j, f in enumerate(feats):
                        src = xin[t][:, :] if f == DENSE_AT else rows[t][:, f, :]
                        mm = pe.transpose(ps_t[k][:, j, :], src, ident[:, :])
                    mm.then_inc(s_tr, 1)

            def select(nxt, k):
                n = nxt.c * N_SEL + k
                pe.wait_ge(s_oh, n + 1)
                if nxt.least >= 1 or k >= 1:
                    pe.wait_ge(s_scopy, n)
                if nxt.least == 0:
                    pe.wait_ge(s_hi, k + 1)
                    pe.wait_ge(s_lo, k + 1)
                slot = onehot[(nxt.par * N_SEL + k) % OH_RING]
                for a in range(SPLIT):
                    for part in (table_hi, table_lo):
                        mm = pe.matmul(ps_s[:, 0:CHUNK], part[k][:, a * DIM:(a + 1) * DIM], slot[0:SEL_K, a, :],
                                       start=(a == 0 and part is table_hi),
                                       stop=(a == SPLIT - 1 and part is table_lo))
                mm.then_inc(s_sel, 1)

            def mlp(c, least, par, r):
                pe.wait_ge(s_mcopy, 1 + MLP_STEPS * c + r)
                if r < M1:
                    if r == 0:
                        for t in range(CHUNK_TILES):
                            pe.wait_ge(s_zr[t], 16 * PAIR_TILES * (c + 1))
                        if least == 0:
                            pe.wait_ge(s_w, 16 * 6)
                    cols = slice(r * 128, (r + 1) * 128)
                    pe.matmul(ps_m[:, 0:CHUNK], w1d_sb[:, cols], denseT[par][:, :], start=True, stop=False)
                    for k in range(PAIR_TILES):
                        mm = pe.matmul(ps_m[:, 0:CHUNK], w1p_sb[:, k, cols], zpair[par][0:PAIR_K, k, :],
                                       start=False, stop=(k == PAIR_TILES - 1))
                elif r < M1 + M2:
                    m = r - M1
                    for k in range(M1):
                        mm = pe.matmul(ps_m[:, 0:CHUNK], w2_sb[:, k, m * 128:(m + 1) * 128], h1[:, k, :],
                                       start=(k == 0), stop=(k == M1 - 1))
                else:
                    for k in range(M2):
                        mm = pe.matmul(ps_m[0:1, 0:CHUNK], w3_sb[:, k:k + 1], h2[:, k, :],
                                       start=(k == 0), stop=(k == M2 - 1))
                mm.then_inc(s_mlp, 1)

            def dots(ch, t):
                for k in range(2):
                    pe.wait_ge(s_tcopy[k], ch.c * N_TGRP + ((t + 1) * N_TGRP + 1 - k) // 2)
                pe.wait_ge(s_scopy, N_SEL * (ch.c + 1))
                for u in range(N_GGRP):
                    if ch.least >= 1 or t >= 1 or u >= 2:
                        pe.wait_ge(s_gcopy[u % 2], (ch.c * CHUNK_TILES + t) * (N_GGRP // 2) + u // 2)
                    for n in range(GRAM_SAMPLES // QUAD):
                        b = u * GRAM_SAMPLES + n * QUAD
                        mm = pe.matmul(ps_g[u % 2][:, n // 4, (n % 4) * GRAM_N:(n % 4 + 1) * GRAM_N],
                                       xT[ch.par][:, t, b:b + QUAD, :].rearrange("p j f -> p (j f)"),
                                       xT[ch.par][:, t, b:b + QUAD, 0:N_FEAT], start=True, stop=True)
                    mm.then_inc(s_gram, 1)

            def body(ch):
                for t in range(CHUNK_TILES):
                    transposes(ch, t)
                    for kind, r in middle_steps(ch, t):
                        if kind == "sel":
                            select(ch.next(), r)
                        else:
                            mlp(ch.c - 1, ch.least - 1, 1 - ch.par, r)
                    dots(ch, t)

            pe.sem_inc(s_mlp, 1)
            pe.wait_ge(s_pad, 1)
            for k in range(N_SEL):
                select(Chunk(0, 0, 0, 0), k)
            pe.wait_ge(s_const, 2)
            chunks(pe, body)
            for r in range(MLP_STEPS):
                mlp(N_CHUNKS - 1, N_CHUNKS - 1, (N_CHUNKS - 1) % 2, r)

        def copy_transposes(copy, eng, ch, t, mine):
            for g, feats in enumerate(T_GROUPS):
                if copier(t, g) != mine:
                    continue
                eng.wait_ge(s_tr, tgroups(ch, t, g) + 1)
                view = xT[ch.par][:, t, :, :].rearrange("p b f -> p f b")
                last = copy(view[:, feats[0]:feats[-1] + 1, :], ps_t[mine][:, 0:len(feats), :])
                if DENSE_AT in feats:
                    last = copy(denseT[ch.par][:, t * TILE:(t + 1) * TILE], ps_t[mine][:, DENSE_AT - feats[0], :])
                last.then_inc(s_tcopy[mine], 1)

        def copy_dots(copy, eng, ch, t, mine):
            q = 32 * t
            if ch.least >= 1:
                eng.wait_ge(s_zw[t], 32 * ch.c)
            for u in range(mine, N_GGRP, 2):
                eng.wait_ge(s_gram, grams(ch, t, u) + 1)
                for j in range(QUAD):
                    src = ps_g[mine][32 * j:32 * j + N_FEAT, :, 0:4 * GRAM_N]\
                        .rearrange("p h (n c) -> p h n c", c=GRAM_N)[:, :, :, j * N_FEAT:(j + 1) * N_FEAT]
                    dst = zsb[q:q + N_FEAT, :].rearrange("p (g u h n j) -> p u j h n g", u=N_GGRP, h=2, n=4, j=QUAD)
                    last = copy(dst[:, u, j, :, :, :], src)
                last.then_inc(s_gcopy[mine], 1)

        @block.scalar
        def _(act):
            def copy(dst, src):
                return act.activation(dst, src, ACT.Copy)

            def copy_selected(nxt, k):
                n = nxt.c * N_SEL + k
                act.wait_ge(s_sel, n + 1)
                copy(xT[nxt.par][:, :, :, DENSE_AT + 1 + k], ps_s[:, 0:CHUNK].rearrange("p (t b) -> p t b", b=TILE))\
                    .then_inc(s_scopy, 1)

            def copy_mlp(c, least, r):
                act.wait_ge(s_mlp, 1 + MLP_STEPS * c + r + 1)
                if r < M1:
                    last = act.activation(h1[:, r, :], ps_m[:, 0:CHUNK], ACT.Relu, bias=b1_sb[:, r:r + 1])
                elif r < M1 + M2:
                    m = r - M1
                    last = act.activation(h2[:, m, :], ps_m[:, 0:CHUNK], ACT.Relu, bias=b2_sb[:, m:m + 1])
                else:
                    act.wait_ge(s_y, 16 * (1 + c))
                    last = copy(y_sb[:, :], ps_m[0:1, 0:CHUNK])
                last.then_inc(s_mcopy, 1)

            def body(ch):
                for t in range(CHUNK_TILES):
                    copy_transposes(copy, act, ch, t, 0)
                    for kind, r in middle_steps(ch, t):
                        if kind == "sel":
                            copy_selected(ch.next(), r)
                        else:
                            copy_mlp(ch.c - 1, ch.least - 1, r)
                    copy_dots(copy, act, ch, t, 0)

            def upper_part(k):
                act.wait_ge(s_raw[k], 16)
                copy(table_hi[k][:, :], table_raw[k % 2]).then_inc(s_hi, 1)

            act.sem_inc(s_mcopy, 1)
            for k in range(2):
                upper_part(k)
            for k in range(N_SEL):
                if k + 2 < N_SEL:
                    upper_part(k + 2)
                copy_selected(Chunk(0, 0, 0, 0), k)
            act.wait_ge(s_w, 16 * 6)
            chunks(act, body)
            for r in range(MLP_STEPS):
                copy_mlp(N_CHUNKS - 1, N_CHUNKS - 1, r)

        @block.vector
        def _(dve):
            def copy(dst, src):
                return dve.tensor_copy(dst, src)

            def lower_part(k):
                dve.wait_ge(s_hi, k + 1)
                dve.tensor_tensor(table_lo[k][:, :], table_raw[k % 2], table_hi[k][:, :].bitcast(F32),
                                  ALU.subtract).then_inc(s_lo, 1)

            def make_onehot(ch, k):
                n = ch.c * N_SEL + k
                if ch.least >= 1 or k >= OH_RING:
                    dve.wait_ge(s_sel, n - OH_RING + 1)
                if k == 0:
                    dve.wait_ge(s_ids[ch.par], 16 * (ch.half + 1))
                slot = onehot[(ch.par * N_SEL + k) % OH_RING]
                for a in range(SPLIT):
                    last = dve.tensor_scalar(slot[0:SEL_K, a, :], ids_row[ch.par][0:SEL_K, k, :],
                                             row_no[0:SEL_K, a:a + 1], None, ALU.is_equal)
                last.then_inc(s_oh, 1)

            def ahead(nxt, k):
                if k + OH_RING < N_SEL:
                    make_onehot(nxt, k + OH_RING)
                else:
                    make_onehot(nxt.next(), k + OH_RING - N_SEL)

            def body(ch):
                for t in range(CHUNK_TILES):
                    copy_transposes(copy, dve, ch, t, 1)
                    for kind, r in middle_steps(ch, t):
                        if kind == "sel":
                            ahead(ch.next(), r)
                    copy_dots(copy, dve, ch, t, 1)

            for p in range(2):
                last = dve.memset(xT[p][:, :, :, N_FEAT:FEAT_PAD], 0.0)
            last.then_inc(s_pad, 1)
            dve.wait_ge(s_const, 1)
            dve.tensor_copy(row_no[:, :], row_no_i[:, :]).then_inc(s_rowno, 1)
            dve.wait_ge(s_rowno, 1)
            first = Chunk(0, 0, 0, 0)
            for k in range(OH_RING):
                lower_part(k)
                make_onehot(first, k)
            for k in range(N_SEL):
                if k + OH_RING < N_SEL:
                    lower_part(k + OH_RING)
                ahead(first, k)
            chunks(dve, body)


def pair_rows():
    first, second = np.triu_indices(N_FEAT, k=1)
    row_of = {(int(a), int(b)): r for r, (a, b) in enumerate(zip(first, second))}
    rows = []
    for f in range(N_FEAT):
        for k in range(1, HALF_FEAT + 1):
            a, b = ORDER[f], ORDER[(f + k) % N_FEAT]
            rows.append(row_of[min(a, b), max(a, b)])
    return np.array(rows)


def kernel(**inputs):
    from concourse import bacc
    from concourse.bass_utils import run_bass_kernel_spmd

    a = {k: np.asarray(v) for k, v in inputs.items()}
    lay = np.ascontiguousarray
    arrays = {
        "ids_gath": lay(a["ids"][:, GATHERED].reshape(BATCH // TILE, TILE, N_GATH)),
        "ids_sel": lay(a["ids"][:, SELECTED].T),
        "x": lay(a["r_dense_x"]),
        **{f"tbl_{t}": lay(a[f"tbl_{t}"]) for t in range(N_TABLES)},
        "w1_pairs": lay(a["W_top1"][pair_rows()]),
        "w1_dense": lay(a["W_top1"][N_PAIRS:]),
        "b1": lay(a["b_top1"].reshape(M1, 128).T),
        "w2": lay(a["W_top2"]),
        "b2": lay(a["b_top2"].reshape(M2, 128).T),
        "w3": lay(a["W_top3"].reshape(M2, 128).T),
    }
    nc = bacc.Bacc("TRN2", target_bir_lowering=False, num_devices=1)
    arrays = {f"in_{n}": v for n, v in arrays.items()}
    dram = {n: nc.dram_tensor(n, v.shape, mybir.dt.from_np(v.dtype), kind="ExternalInput").ap() for n, v in arrays.items()}
    out = nc.dram_tensor("out_y", (BATCH, 1), F32, kind="ExternalOutput").ap()
    d = lambda n: dram[f"in_{n}"]
    build(nc, d("ids_gath"), d("ids_sel"), d("x"), [d(f"tbl_{t}") for t in range(N_TABLES)],
          d("w1_pairs"), d("w1_dense"), d("b1"), d("w2"), d("b2"), d("w3"), out)
    r = run_bass_kernel_spmd(nc, [arrays], core_ids=[0])
    return r.results[0]["out_y"]
```

```python
import numpy as np
import concourse.bass as bass
import concourse.mybir as mybir
from contextlib import ExitStack

F32 = mybir.dt.float32
F32R = mybir.dt.float32r
I32 = mybir.dt.int32
U32 = mybir.dt.uint32
ALU = mybir.AluOpType
ACT = mybir.ActivationFunctionType

BATCH, DIM = 2048, 128
N_TABLES = 26
N_FEAT = N_TABLES + 1
SELECTED = [2, 5, 7, 10, 11, 12]
GATHERED = [t for t in range(N_TABLES) if t not in SELECTED]
SEL_ROWS = 1000
N_SEL, N_GATH = len(SELECTED), len(GATHERED)
ORDER = GATHERED + [N_TABLES] + SELECTED
DENSE_AT = N_GATH

TILE = 128
CHUNK_TILES = 2
CHUNK = TILE * CHUNK_TILES
N_CHUNKS = BATCH // CHUNK

SPLIT = 8
SEL_K = SEL_ROWS // SPLIT
OH_RING = 2

BANK_FEATS = 4
N_TGRP = -(-(N_GATH + 1) // BANK_FEATS)
T_GROUPS = [list(range(BANK_FEATS * g, min(BANK_FEATS * (g + 1), N_GATH + 1))) for g in range(N_TGRP)]

HALF_FEAT = N_FEAT // 2
N_PAIRS = N_FEAT * HALF_FEAT
Z_COLS = N_FEAT + HALF_FEAT
PAIR_TILES = 3
F_PER_TILE = N_FEAT // PAIR_TILES
PAIR_K = F_PER_TILE * HALF_FEAT

QUAD = 4
GRAM_SAMPLES = 32
N_GGRP = TILE // GRAM_SAMPLES
GRAM_N = QUAD * N_FEAT
FEAT_PAD = 32

H1, H2 = 512, 256
M1, M2 = H1 // 128, H2 // 128
MLP_STEPS = M1 + M2 + 1

SEL_CUT = N_SEL // 2
MLP_CUT = 3
PATTERN = [
    "place sel tr sel tr dots sel tr dots sel mlp tr dots mlp tr dots mlp tr".split(),
    "sel tr mlp sel dots tr sel mlp dots place tr mlp dots tr mlp dots tr".split(),
]
LAST_PATTERN = [
    "place tr mlp tr dots mlp tr dots tr dots tr dots mlp".split(),
    "dots dots dots dots".split(),
]


class Chunk:

    def __init__(self, number, half, parity, least):
        self.c = number
        self.half = half
        self.par = parity
        self.least = least

    def next(self):
        return Chunk(self.c + 1, self.half + self.par, 1 - self.par, self.least + 1)


FIRST = Chunk(0, 0, 0, 0)


def build(nc, ids_gath, ids_sel, x, tables, w1_pairs, w1_dense, b1, w2, b2, w3, out):
    ctx = ExitStack()
    with ctx:
        def sb(name, shape, dt=F32):
            return ctx.enter_context(nc.sbuf_tensor(name, shape, dt))

        def sem(name):
            return ctx.enter_context(nc.semaphore(name))

        ident = sb("ident", [128, 128])
        idx = [sb(f"idx{p}", [128, CHUNK_TILES, N_GATH], I32) for p in range(2)]
        ids_row = [sb(f"ids_row{p}", [128, N_SEL, CHUNK], I32) for p in range(2)]
        rows = [sb(f"rows{t}", [128, N_GATH, DIM]) for t in range(CHUNK_TILES)]
        xin = [sb(f"xin{t}", [128, DIM]) for t in range(CHUNK_TILES)]
        table_hi = [sb(f"table_hi{k}", [SEL_K, SPLIT * DIM], F32R) for k in range(N_SEL)]
        table_lo = [sb(f"table_lo{k}", [SEL_K, SPLIT * DIM], F32R) for k in range(N_SEL)]
        row_no_i = sb("row_no_i", [128, SPLIT], I32)
        row_no = sb("row_no", [128, SPLIT])
        onehot = [sb(f"onehot{k}", [128, SPLIT, CHUNK], F32R) for k in range(OH_RING)]
        picked = [sb(f"picked{p}", [128, N_SEL, CHUNK]) for p in range(2)]
        xT = [sb(f"xT{t}", [128, TILE, FEAT_PAD]) for t in range(CHUNK_TILES)]
        denseT = [sb(f"denseT{p}", [128, CHUNK]) for p in range(2)]
        zsb = sb("zsb", [128, N_FEAT * TILE])
        table_raw = [zsb[0:SEL_K, k * SPLIT * DIM:(k + 1) * SPLIT * DIM] for k in range(2)]
        zpair = [sb(f"zpair{p}", [128, PAIR_TILES, CHUNK]) for p in range(2)]
        w1p_sb = sb("w1p_sb", [PAIR_K, PAIR_TILES, H1])
        w1d_sb = sb("w1d_sb", [128, H1])
        w2_sb = sb("w2_sb", [128, M1, H2])
        w3_sb = sb("w3_sb", [128, M2])
        b1_sb = sb("b1_sb", [128, M1])
        b2_sb = sb("b2_sb", [128, M2])
        h1 = sb("h1", [128, M1, CHUNK])
        h2 = sb("h2", [128, M2, CHUNK])
        y_sb = sb("y_sb", [1, CHUNK])

        ps_t = [ctx.enter_context(nc.psum_tensor(f"ps_t{k}", [128, BANK_FEATS, TILE], F32)) for k in range(2)]
        ps_g = [ctx.enter_context(nc.psum_tensor(f"ps_g{k}", [128, 2, 512], F32)) for k in range(2)]
        ps_s = ctx.enter_context(nc.psum_tensor("ps_s", [128, 512], F32))
        ps_m = ctx.enter_context(nc.psum_tensor("ps_m", [128, 512], F32))

        z_dram = [nc.dram_tensor(f"z_dram{t}", [N_FEAT, Z_COLS * TILE], F32, kind="Internal") for t in range(CHUNK_TILES)]

        s_zero = sem("s_zero")
        s_const = sem("s_const")
        s_rowno = sem("s_rowno")
        s_pad = sem("s_pad")
        s_raw = [sem(f"s_raw{k}") for k in range(N_SEL)]
        s_hi = sem("s_hi")
        s_lo = sem("s_lo")
        s_w = sem("s_w")
        s_idx = [sem(f"s_idx{p}") for p in range(2)]
        s_ids = [sem(f"s_ids{p}") for p in range(2)]
        s_x = [sem(f"s_x{t}") for t in range(CHUNK_TILES)]
        s_place = sem("s_place")
        s_rows = [[sem(f"s_rows{t}_{g}") for g in range(N_TGRP)] for t in range(CHUNK_TILES)]
        s_tr = sem("s_tr")
        s_tcopy = [sem(f"s_tcopy{k}") for k in range(2)]
        s_oh = sem("s_oh")
        s_sel = sem("s_sel")
        s_scopy = sem("s_scopy")
        s_place_sel = sem("s_place_sel")
        s_gram = sem("s_gram")
        s_gcopy = [sem(f"s_gcopy{k}") for k in range(2)]
        s_zw = [sem(f"s_zw{t}") for t in range(CHUNK_TILES)]
        s_zr = [sem(f"s_zr{t}") for t in range(CHUNK_TILES)]
        s_mlp = sem("s_mlp")
        s_mcopy = sem("s_mcopy")
        s_y = sem("s_y")

        block = ctx.enter_context(nc.Block())

        def chunks(eng, body):
            body(FIRST)
            with eng.Fori(0, (N_CHUNKS - 2) // 2) as i:
                first = Chunk(i * 2 + 1, i, 1, 1)
                body(first)
                body(first.next())
            body(Chunk(N_CHUNKS - 1, (N_CHUNKS - 1) // 2, (N_CHUNKS - 1) % 2, N_CHUNKS - 1))

        def period(ch, t):
            last = ch.least == N_CHUNKS - 1
            steps = {
                "place": [] if last and t == 1 else [0],
                "tr": [] if last and t == 1 else list(range(N_TGRP)),
                "sel": [] if last else list(range(SEL_CUT)) if t == 0 else list(range(SEL_CUT, N_SEL)),
                "mlp": [] if ch.least == 0 else list(range(MLP_CUT)) if t == 0 else list(range(MLP_CUT, MLP_STEPS)),
                "dots": list(range(N_GGRP)),
            }
            order = (LAST_PATTERN if last else PATTERN)[t]
            return [(kind, steps[kind].pop(0)) for kind in order if steps[kind]] + \
                [(kind, n) for kind, left in steps.items() for n in left]

        def opening():
            steps = [("sel", 0), ("sel", 1)]
            for n in range(max(N_SEL - 2, N_TGRP)):
                steps += [("tr", n)] * (n < N_TGRP) + [("sel", n + 2)] * (n + 2 < N_SEL)
            return steps + [("place", 0)]

        def closing(t):
            return [(MLP_STEPS * (N_CHUNKS - 1 + t) + r, r) for r in range(MLP_STEPS)]

        def late(ch, r):
            return r + 1 if ch.least == N_CHUNKS - 1 else 0

        def next_tile(ch, t):
            return (ch, 1) if t == 0 else (ch.next(), 0)

        def copier(t, g):
            return (t * N_TGRP + g) % 2

        def bank_use(ch, t, g):
            return ch.c * N_TGRP + (t * N_TGRP + g) // 2

        def tgroups(ch, t, g):
            return (ch.c * CHUNK_TILES + t) * N_TGRP + g

        def grams(ch, t, u):
            return (ch.c * CHUNK_TILES + t) * N_GGRP + u

        @block.sync
        def _(sp):
            def load_idx(first_tile, par):
                sp.dma_start(idx[par][:, :, :], ids_gath[bass.ds(first_tile, CHUNK_TILES), :, :]
                             .rearrange("t p f -> p t f")).then_inc(s_idx[par], 16)

            def load_ids(sample, par):
                sp.dma_start(ids_row[par][:, :, :],
                             ids_sel[:, bass.ds(sample, CHUNK)].partition_broadcast(128)).then_inc(s_ids[par], 16)

            def load_x(sample, t):
                sp.dma_start(xin[t][:, :], x[bass.ds(sample, TILE), :]).then_inc(s_x[t], 16)

            sp.sem_inc(s_y, 16)
            load_idx(0, 0)
            load_ids(0, 0)
            load_idx(CHUNK_TILES, 1)
            for t in range(CHUNK_TILES):
                load_x(t * TILE, t)
            load_ids(CHUNK, 1)
            for k in range(2, N_SEL):
                sp.wait_ge(s_lo, k - 1)
                sp.dma_start(table_raw[k % 2], tables[SELECTED[k]].rearrange("(p a) d -> p (a d)", a=SPLIT))\
                  .then_inc(s_raw[k], 16)
            for dst, src in ((w1p_sb[:, :, :], w1_pairs.rearrange("(k p) n -> p k n", p=PAIR_K)),
                             (w1d_sb[:, :], w1_dense), (w2_sb[:, :, :], w2.rearrange("(k p) n -> p k n", p=128)),
                             (w3_sb[:, :], w3), (b1_sb[:, :], b1), (b2_sb[:, :], b2)):
                sp.dma_start(dst, src).then_inc(s_w, 16)

            def bounce(ch, t, copied, read, written, layer_done):
                sp.wait_ge(s_gcopy[0], copied)
                sp.wait_ge(s_gcopy[1], copied)
                if ch.least >= 1:
                    sp.wait_ge(s_zr[t], read)
                q = 32 * t
                sp.dma_start(z_dram[t][:, 0:N_FEAT * TILE], zsb[q:q + N_FEAT, :]).then_inc(s_zw[t], 16)
                sp.dma_start(z_dram[t][:, N_FEAT * TILE:Z_COLS * TILE], zsb[q:q + N_FEAT, 0:HALF_FEAT * TILE])\
                  .then_inc(s_zw[t], 16)
                sp.wait_ge(s_zw[t], written)
                if ch.least >= 1:
                    sp.wait_ge(s_mlp, layer_done)
                base = z_dram[t][:, :]
                for k in range(PAIR_TILES):
                    f0 = k * F_PER_TILE
                    diagonal = bass.AP(tensor=base.tensor, offset=(f0 * Z_COLS + f0 + 1) * TILE,
                                       ap=[[(Z_COLS + 1) * TILE, F_PER_TILE], [TILE, HALF_FEAT], [1, TILE]])
                    sp.dma_start(zpair[ch.par][0:PAIR_K, k, t * TILE:(t + 1) * TILE], diagonal)\
                      .then_inc(s_zr[t], 16)

            def store_y(copied, sample):
                sp.wait_ge(s_mcopy, copied)
                sp.dma_start(out[bass.ds(sample, CHUNK), :].rearrange("n o -> o n"), y_sb[:, :]).then_inc(s_y, 16)

            def held(value):
                if isinstance(value, int):
                    return value
                reg = sp.alloc_register(f"held{len(held_regs)}")
                held_regs.append(reg)
                sp.reg_mov(reg, value)
                return sp.snap(reg)

            held_regs = []

            def body(ch):
                not_last = ch.least < N_CHUNKS - 1
                if not_last:
                    x0, x1 = (ch.c + 1) * CHUNK, (ch.c + 1) * CHUNK + TILE
                    far_sample, far_tile = (ch.c + 2) % N_CHUNKS * CHUNK, (ch.c + 2) % N_CHUNKS * CHUNK_TILES
                if ch.least >= 1:
                    y0 = (ch.c - 1) * CHUNK
                ids_used = held(N_SEL * (ch.c + 1))
                transposed = [held(tgroups(ch, t + 1, 0)) for t in range(CHUNK_TILES)]
                y_copied = held(1 + MLP_STEPS * ch.c)
                counts = [held(16 * PAIR_TILES * ch.c), held(32 * (ch.c + 1)), held(1 + MLP_STEPS * (ch.c - 1))]
                copied = [held((ch.c * CHUNK_TILES + t + 1) * (N_GGRP // 2)) for t in range(CHUNK_TILES)]
                if not_last:
                    sp.wait_ge(s_oh, ids_used)
                    load_ids(far_sample, ch.par)
                    sp.wait_ge(s_tr, transposed[0])
                    load_x(x0, 0)
                bounce(ch, 0, copied[0], *counts)
                if not_last:
                    sp.wait_ge(s_tr, transposed[1])
                    load_x(x1, 1)
                    load_idx(far_tile, ch.par)
                bounce(ch, 1, copied[1], *counts)
                if ch.least >= 1:
                    store_y(y_copied, y0)

            chunks(sp, body)
            store_y(1 + MLP_STEPS * (N_CHUNKS + 1), BATCH - CHUNK)
            sp.wait_ge(s_y, 16 * (1 + N_CHUNKS))
            for p in range(2):
                sp.wait_ge(s_idx[p], 16 * (1 + (N_CHUNKS - p) // 2))
                sp.wait_ge(s_ids[p], 16 * (1 + (N_CHUNKS - p) // 2))

        @block.gpsimd
        def _(pool):
            pool.iota(row_no_i[:, :], pattern=[[1, SPLIT]], base=0, channel_multiplier=SPLIT).then_inc(s_const, 1)
            pool.memset(ident[:, :], 0.0).then_inc(s_zero, 1)
            pool.wait_ge(s_zero, 1)
            pool.affine_select(out=ident[:, :], in_=ident[:, :], compare_op=ALU.not_equal, fill=1.0,
                               base=0, pattern=[[-1, 128]], channel_multiplier=1).then_inc(s_const, 1)

            def body(ch):
                pool.wait_ge(s_idx[ch.par], 16 * (ch.half + 1))
                for t in range(CHUNK_TILES):
                    for g, feats in enumerate(T_GROUPS):
                        if ch.least >= 1:
                            pool.wait_ge(s_tr, tgroups(ch, t, g) - CHUNK_TILES * N_TGRP + 1)
                            pool.sem_inc(s_place, 1)
                        for f in feats:
                            if f != DENSE_AT:
                                pool.indirect_dma_start(
                                    rows[t][:, f, :], None, tables[GATHERED[f]][:, :],
                                    bass.IndirectOffsetOnAxis(ap=idx[ch.par][:, t, f:f + 1].bitcast(U32), axis=0),
                                ).then_inc(s_rows[t][g], 16)

            chunks(pool, body)

        @block.tensor
        def _(pe):
            def transposes(ch, t, g):
                feats = T_GROUPS[g]
                n_rows = len([f for f in feats if f != DENSE_AT])
                if n_rows:
                    pe.wait_ge(s_rows[t][g], 16 * n_rows * (ch.c + 1))
                if DENSE_AT in feats:
                    pe.wait_ge(s_x[t], 16 * (ch.c + 1))
                k = copier(t, g)
                if ch.least >= 1 or (t * N_TGRP + g) // 2 >= 1:
                    pe.wait_ge(s_tcopy[k], bank_use(ch, t, g))
                for j, f in enumerate(feats):
                    src = xin[t][:, :] if f == DENSE_AT else rows[t][:, f, :]
                    mm = pe.transpose(ps_t[k][:, j, :], src, ident[:, :])
                mm.then_inc(s_tr, 1)

            def select(nxt, k):
                n = nxt.c * N_SEL + k
                pe.wait_ge(s_oh, n + 1)
                if nxt.least >= 1 or k >= 1:
                    pe.wait_ge(s_scopy, n)
                if nxt.least == 0:
                    pe.wait_ge(s_hi, k + 1)
                    pe.wait_ge(s_lo, k + 1)
                slot = onehot[(nxt.par * N_SEL + k) % OH_RING]
                for a in range(SPLIT):
                    for part in (table_hi, table_lo):
                        mm = pe.matmul(ps_s[:, 0:CHUNK], part[k][:, a * DIM:(a + 1) * DIM], slot[0:SEL_K, a, :],
                                       start=(a == 0 and part is table_hi),
                                       stop=(a == SPLIT - 1 and part is table_lo))
                mm.then_inc(s_sel, 1)

            def mlp(done, par, r, tiles, filled, late):
                if late <= 1 or r in (M1, M1 + M2):
                    pe.wait_ge(s_mcopy, 1 + done)
                else:
                    pe.wait_ge(s_mcopy, done)
                bank = ps_s if late and late % 2 == 0 else ps_m
                if r == 0:
                    for t in tiles:
                        pe.wait_ge(s_zr[t], 16 * PAIR_TILES * filled)
                cols = slice(tiles[0] * TILE, (tiles[-1] + 1) * TILE)
                o = bank[:, cols]
                if r < M1:
                    w = slice(r * 128, (r + 1) * 128)
                    pe.matmul(o, w1d_sb[:, w], denseT[par][:, cols], start=True, stop=False)
                    for k in range(PAIR_TILES):
                        mm = pe.matmul(o, w1p_sb[:, k, w], zpair[par][0:PAIR_K, k, cols],
                                       start=False, stop=(k == PAIR_TILES - 1))
                elif r < M1 + M2:
                    m = r - M1
                    for k in range(M1):
                        mm = pe.matmul(o, w2_sb[:, k, m * 128:(m + 1) * 128], h1[:, k, cols],
                                       start=(k == 0), stop=(k == M1 - 1))
                else:
                    for k in range(M2):
                        mm = pe.matmul(bank[0:1, cols], w3_sb[:, k:k + 1], h2[:, k, cols],
                                       start=(k == 0), stop=(k == M2 - 1))
                mm.then_inc(s_mlp, 1)

            def dots(ch, t, u):
                if u == 0:
                    for k in range(2):
                        pe.wait_ge(s_tcopy[k], ch.c * N_TGRP + ((t + 1) * N_TGRP + 1 - k) // 2)
                    pe.wait_ge(s_place_sel, ch.c * CHUNK_TILES + t + 1)
                if ch.least >= 1 or t >= 1 or u >= 2:
                    pe.wait_ge(s_gcopy[u % 2], (ch.c * CHUNK_TILES + t) * (N_GGRP // 2) + u // 2)
                for n in range(GRAM_SAMPLES // QUAD):
                    b = u * GRAM_SAMPLES + n * QUAD
                    mm = pe.matmul(ps_g[u % 2][:, n // 4, (n % 4) * GRAM_N:(n % 4 + 1) * GRAM_N],
                                   xT[t][:, b:b + QUAD, :].rearrange("p j f -> p (j f)"),
                                   xT[t][:, b:b + QUAD, 0:N_FEAT], start=True, stop=True)
                mm.then_inc(s_gram, 1)

            def body(ch):
                for t in range(CHUNK_TILES):
                    for kind, n in period(ch, t):
                        if kind == "tr":
                            transposes(*next_tile(ch, t), n)
                        elif kind == "sel":
                            select(ch.next(), n)
                        elif kind == "mlp":
                            mlp(MLP_STEPS * (ch.c - 1) + n, 1 - ch.par, n, range(CHUNK_TILES), ch.c, late(ch, n))
                        elif kind == "dots":
                            dots(ch, t, n)

            pe.sem_inc(s_mlp, 1)
            pe.wait_ge(s_pad, 1)
            pe.wait_ge(s_const, 2)
            for kind, n in opening():
                if kind == "tr":
                    transposes(FIRST, 0, n)
                elif kind == "sel":
                    select(FIRST, n)
            pe.wait_ge(s_w, 16 * 6)
            chunks(pe, body)
            for t in range(CHUNK_TILES):
                for done, r in closing(t):
                    mlp(done, (N_CHUNKS - 1) % 2, r, [t], N_CHUNKS, MLP_STEPS * (1 + t) + r + 1)

        def copy_transposes(copy, eng, ch, t, g, mine):
            feats = T_GROUPS[g]
            eng.wait_ge(s_tr, tgroups(ch, t, g) + 1)
            last = copy(xT[t].rearrange("p b f -> p f b")[:, feats[0]:feats[-1] + 1, :], ps_t[mine][:, 0:len(feats), :])
            if DENSE_AT in feats:
                last = copy(denseT[ch.par][:, t * TILE:(t + 1) * TILE], ps_t[mine][:, DENSE_AT - feats[0], :])
            last.then_inc(s_tcopy[mine], 1)

        def copy_dots(copy, eng, ch, t, u, mine):
            q = 32 * t
            if ch.least >= 1 and u < 2:
                eng.wait_ge(s_zw[t], 32 * ch.c)
            eng.wait_ge(s_gram, grams(ch, t, u) + 1)
            dst = zsb[q:q + N_FEAT, :].rearrange("p (g u h n j) -> p u j h n g", u=N_GGRP, h=2, n=4, j=QUAD)
            for j in range(QUAD):
                src = ps_g[mine][32 * j:32 * j + N_FEAT, :, 0:4 * GRAM_N]\
                    .rearrange("p h (n c) -> p h n c", c=GRAM_N)[:, :, :, j * N_FEAT:(j + 1) * N_FEAT]
                last = copy(dst[:, u, j, :, :, :], src)
            last.then_inc(s_gcopy[mine], 1)

        @block.scalar
        def _(act):
            def copy(dst, src):
                return act.activation(dst, src, ACT.Copy)

            def copy_selected(nxt, k):
                act.wait_ge(s_sel, nxt.c * N_SEL + k + 1)
                copy(picked[nxt.par][:, k, :], ps_s[:, 0:CHUNK]).then_inc(s_scopy, 1)

            def copy_mlp(done, r, tiles, c, late):
                act.wait_ge(s_mlp, 1 + done + 1)
                bank = ps_s if late and late % 2 == 0 else ps_m
                cols = slice(tiles[0] * TILE, (tiles[-1] + 1) * TILE)
                if r < M1:
                    last = act.activation(h1[:, r, cols], bank[:, cols], ACT.Relu, bias=b1_sb[:, r:r + 1])
                elif r < M1 + M2:
                    m = r - M1
                    last = act.activation(h2[:, m, cols], bank[:, cols], ACT.Relu, bias=b2_sb[:, m:m + 1])
                else:
                    act.wait_ge(s_y, 16 * (1 + c))
                    last = copy(y_sb[:, cols], bank[0:1, cols])
                last.then_inc(s_mcopy, 1)

            def body(ch):
                for t in range(CHUNK_TILES):
                    for kind, n in period(ch, t):
                        if kind == "tr":
                            nxt, nt = next_tile(ch, t)
                            if copier(nt, n) == 0:
                                copy_transposes(copy, act, nxt, nt, n, 0)
                        elif kind == "sel":
                            copy_selected(ch.next(), n)
                        elif kind == "mlp":
                            copy_mlp(MLP_STEPS * (ch.c - 1) + n, n, range(CHUNK_TILES), ch.c - 1, late(ch, n))
                        elif kind == "dots" and n % 2 == 0:
                            copy_dots(copy, act, ch, t, n, 0)

            def upper_part(k):
                act.wait_ge(s_raw[k], 16)
                copy(table_hi[k][:, :], table_raw[k % 2]).then_inc(s_hi, 1)

            act.sem_inc(s_mcopy, 1)
            for k in range(2):
                act.dma_start(table_raw[k], tables[SELECTED[k]].rearrange("(p a) d -> p (a d)", a=SPLIT))\
                    .then_inc(s_raw[k], 16)
            for k in range(2):
                upper_part(k)
            for kind, n in opening():
                if kind == "tr" and copier(0, n) == 0:
                    copy_transposes(copy, act, FIRST, 0, n, 0)
                elif kind == "sel":
                    if n + 2 < N_SEL:
                        upper_part(n + 2)
                    copy_selected(FIRST, n)
            act.wait_ge(s_w, 16 * 6)
            chunks(act, body)
            for t in range(CHUNK_TILES):
                for done, r in closing(t):
                    copy_mlp(done, r, [t], N_CHUNKS - 1, MLP_STEPS * (1 + t) + r + 1)

        @block.vector
        def _(dve):
            def copy(dst, src):
                return dve.tensor_copy(dst, src)

            def lower_part(k):
                dve.wait_ge(s_hi, k + 1)
                dve.tensor_tensor(table_lo[k][:, :], table_raw[k % 2], table_hi[k][:, :].bitcast(F32),
                                  ALU.subtract).then_inc(s_lo, 1)

            def make_onehot(ch, k):
                n = ch.c * N_SEL + k
                if ch.least >= 1 or k >= OH_RING:
                    dve.wait_ge(s_sel, n - OH_RING + 1)
                if k == 0:
                    dve.wait_ge(s_ids[ch.par], 16 * (ch.half + 1))
                slot = onehot[(ch.par * N_SEL + k) % OH_RING]
                for a in range(SPLIT):
                    last = dve.tensor_scalar(slot[0:SEL_K, a, :], ids_row[ch.par][0:SEL_K, k, :],
                                             row_no[0:SEL_K, a:a + 1], None, ALU.is_equal)
                last.then_inc(s_oh, 1)

            def ahead(nxt, k):
                if k + OH_RING < N_SEL:
                    make_onehot(nxt, k + OH_RING)
                else:
                    make_onehot(nxt.next(), k + OH_RING - N_SEL)

            def place_selected(ch, t):
                dve.wait_ge(s_scopy, N_SEL * (ch.c + 1))
                if ch.least >= 1:
                    dve.wait_ge(s_gram, grams(ch, t, 0) - CHUNK_TILES * N_GGRP + N_GGRP)
                dve.tensor_copy(xT[t].rearrange("p b f -> p f b")[:, DENSE_AT + 1:N_FEAT, :],
                                picked[ch.par][:, :, t * TILE:(t + 1) * TILE]).then_inc(s_place_sel, 1)

            def body(ch):
                for t in range(CHUNK_TILES):
                    nxt, nt = next_tile(ch, t)
                    for kind, n in period(ch, t):
                        if kind == "place":
                            place_selected(nxt, nt)
                        elif kind == "tr" and copier(nt, n) == 1:
                            copy_transposes(copy, dve, nxt, nt, n, 1)
                        elif kind == "sel":
                            ahead(ch.next(), n)
                        elif kind == "dots" and n % 2 == 1:
                            copy_dots(copy, dve, ch, t, n, 1)

            for t in range(CHUNK_TILES):
                last = dve.memset(xT[t][:, :, N_FEAT:FEAT_PAD], 0.0)
            last.then_inc(s_pad, 1)
            dve.wait_ge(s_const, 1)
            dve.tensor_copy(row_no[:, :], row_no_i[:, :]).then_inc(s_rowno, 1)
            dve.wait_ge(s_rowno, 1)
            for k in range(OH_RING):
                make_onehot(FIRST, k)
                lower_part(k)
            for kind, n in opening():
                if kind == "tr" and copier(0, n) == 1:
                    copy_transposes(copy, dve, FIRST, 0, n, 1)
                elif kind == "sel":
                    if n + OH_RING < N_SEL:
                        lower_part(n + OH_RING)
                    ahead(FIRST, n)
                elif kind == "place":
                    place_selected(FIRST, 0)
            chunks(dve, body)


def pair_rows():
    first, second = np.triu_indices(N_FEAT, k=1)
    row_of = {(int(a), int(b)): r for r, (a, b) in enumerate(zip(first, second))}
    rows = []
    for f in range(N_FEAT):
        for k in range(1, HALF_FEAT + 1):
            a, b = ORDER[f], ORDER[(f + k) % N_FEAT]
            rows.append(row_of[min(a, b), max(a, b)])
    return np.array(rows)


def kernel(**inputs):
    from concourse import bacc
    from concourse.bass_utils import run_bass_kernel_spmd

    a = {k: np.asarray(v) for k, v in inputs.items()}
    lay = np.ascontiguousarray
    arrays = {
        "ids_gath": lay(a["ids"][:, GATHERED].reshape(BATCH // TILE, TILE, N_GATH)),
        "ids_sel": lay(a["ids"][:, SELECTED].T),
        "x": lay(a["r_dense_x"]),
        **{f"tbl_{t}": lay(a[f"tbl_{t}"]) for t in range(N_TABLES)},
        "w1_pairs": lay(a["W_top1"][pair_rows()]),
        "w1_dense": lay(a["W_top1"][N_PAIRS:]),
        "b1": lay(a["b_top1"].reshape(M1, 128).T),
        "w2": lay(a["W_top2"]),
        "b2": lay(a["b_top2"].reshape(M2, 128).T),
        "w3": lay(a["W_top3"].reshape(M2, 128).T),
    }
    nc = bacc.Bacc("TRN2", target_bir_lowering=False, num_devices=1)
    arrays = {f"in_{n}": v for n, v in arrays.items()}
    dram = {n: nc.dram_tensor(n, v.shape, mybir.dt.from_np(v.dtype), kind="ExternalInput").ap() for n, v in arrays.items()}
    out = nc.dram_tensor("out_y", (BATCH, 1), F32, kind="ExternalOutput").ap()
    d = lambda n: dram[f"in_{n}"]
    build(nc, d("ids_gath"), d("ids_sel"), d("x"), [d(f"tbl_{t}") for t in range(N_TABLES)],
          d("w1_pairs"), d("w1_dense"), d("b1"), d("w2"), d("b2"), d("w3"), out)
    r = run_bass_kernel_spmd(nc, [arrays], core_ids=[0])
    return r.results[0]["out_y"]
```

```python
import numpy as np
import concourse.bass as bass
import concourse.mybir as mybir
from contextlib import ExitStack

F32 = mybir.dt.float32
F32R = mybir.dt.float32r
I32 = mybir.dt.int32
U32 = mybir.dt.uint32
ALU = mybir.AluOpType
ACT = mybir.ActivationFunctionType

BATCH, DIM = 2048, 128
N_TABLES = 26
N_FEAT = N_TABLES + 1
SELECTED = [2, 5, 7, 10, 11, 12]
SHARED = [22, 24]
GATHERED = [t for t in range(N_TABLES) if t not in SELECTED + SHARED]
SEL_ROWS = 1000
N_SEL, N_SHARED, N_GATH = len(SELECTED), len(SHARED), len(GATHERED)
N_ON_CHIP = N_SEL + N_SHARED
ORDER = GATHERED + [N_TABLES] + SHARED + SELECTED
DENSE_AT = N_GATH

TILE = 128
CHUNK_TILES = 2
CHUNK = TILE * CHUNK_TILES
N_CHUNKS = BATCH // CHUNK

SPLIT = 8
SEL_K = SEL_ROWS // SPLIT
RAW_BUFS = 3
OH_AHEAD = 2

BANK_FEATS = 4
T_GROUPS = [[list(range(f, min(f + BANK_FEATS, n))) for f in range(0, n, BANK_FEATS)]
            for n in (N_GATH + 1 + N_SHARED, N_GATH + 1)]
N_TGRP = [len(groups) for groups in T_GROUPS]

HALF_FEAT = N_FEAT // 2
N_PAIRS = N_FEAT * HALF_FEAT
Z_COLS = N_FEAT + HALF_FEAT
PAIR_TILES = 3
F_PER_TILE = N_FEAT // PAIR_TILES
PAIR_K = F_PER_TILE * HALF_FEAT

QUAD = 4
GRAM_SAMPLES = 32
N_GGRP = TILE // GRAM_SAMPLES
GRAM_N = QUAD * N_FEAT
FEAT_PAD = 32
GRAM_M = (QUAD - 1) * FEAT_PAD + N_FEAT

H1, H2 = 512, 256
M1, M2 = H1 // 128, H2 // 128
MLP_STEPS = M1 + M2 + 1

SEL_CUT = 4
PATTERN = [
    "place sel dots sel tr dots sel tr mlp sel tr dots mlp tr dots mlp tr".split(),
    "sel mlp tr sel dots mlp tr sel dots mlp tr sel place dots mlp tr dots tr tr".split(),
]
MLP_CUT = PATTERN[0].count("mlp")
LAST_PATTERN = [
    "place tr dots tr dots dots tr dots mlp mlp tr mlp tr mlp tr".split(),
    "dots dots dots dots".split(),
]
LAST_MLP_CUT = M1


class Chunk:

    def __init__(self, number, half, parity, least):
        self.c = number
        self.half = half
        self.par = parity
        self.least = least

    def n_sel(self):
        return N_SEL + N_SHARED * self.par

    def sels(self):
        return self.c * N_SEL + self.half * N_SHARED

    def tgroups(self, t=0, g=0):
        return self.half * (CHUNK_TILES * sum(N_TGRP)) + (self.par * CHUNK_TILES * N_TGRP[0] + t * N_TGRP[self.par] + g)

    def next(self):
        return Chunk(self.c + 1, self.half + self.par, 1 - self.par, self.least + 1)


FIRST = Chunk(0, 0, 0, 0)


def build(nc, ids_gath, ids_sel, x, tables, w1_pairs, w1_dense, b1, w2, b2, w3, out):
    ctx = ExitStack()
    with ctx:
        def sb(name, shape, dt=F32):
            return ctx.enter_context(nc.sbuf_tensor(name, shape, dt))

        def sem(name):
            return ctx.enter_context(nc.semaphore(name))

        ident = sb("ident", [128, 128])
        idx = [sb(f"idx{p}", [128, CHUNK_TILES, N_GATH + N_SHARED], I32) for p in range(2)]
        ids_row = [sb(f"ids_row{p}", [128, N_ON_CHIP, CHUNK], I32) for p in range(2)]
        rows = [sb(f"rows{t}", [128, N_GATH + 1 + N_SHARED, DIM]) for t in range(CHUNK_TILES)]
        table_hi = [sb(f"table_hi{k}", [SEL_K, SPLIT * DIM], F32R) for k in range(N_ON_CHIP)]
        table_lo = [sb(f"table_lo{k}", [SEL_K, SPLIT * DIM], F32R) for k in range(N_ON_CHIP)]
        row_no_i = sb("row_no_i", [128, SPLIT], I32)
        row_no = sb("row_no", [128, SPLIT])
        onehot = [sb(f"onehot{k}", [128, SPLIT, CHUNK], F32R) for k in range(2 + N_SHARED % 2)]
        picked = [sb(f"picked{p}", [128, N_ON_CHIP, CHUNK]) for p in range(2)]
        xT = [sb(f"xT{t}", [128, TILE, FEAT_PAD]) for t in range(CHUNK_TILES)]
        denseT = [sb(f"denseT{p}", [128, CHUNK]) for p in range(2)]
        zsb = sb("zsb", [128, N_FEAT * TILE])
        zpair = [sb(f"zpair{p}", [128, PAIR_TILES, CHUNK]) for p in range(2)]
        w1p_sb = sb("w1p_sb", [PAIR_K, PAIR_TILES, H1])
        w1d_sb = sb("w1d_sb", [128, H1])
        w2_sb = sb("w2_sb", [128, M1, H2])
        w3_sb = sb("w3_sb", [128, M2])
        b1_sb = sb("b1_sb", [128, M1])
        b2_sb = sb("b2_sb", [128, M2])
        h1 = sb("h1", [128, M1, CHUNK])
        h2 = sb("h2", [128, M2, CHUNK])
        y_sb = sb("y_sb", [1, CHUNK])
        zsb_raw = [zsb[0:SEL_K, k * SPLIT * DIM:(k + 1) * SPLIT * DIM] for k in range(RAW_BUFS)]
        table_raw = [zsb_raw[k % RAW_BUFS] if k < N_SEL else h1.rearrange("p m c -> p (m c)")[0:SEL_K, 0:SPLIT * DIM]
                     for k in range(N_ON_CHIP)]

        ps_t = [ctx.enter_context(nc.psum_tensor(f"ps_t{k}", [128, BANK_FEATS, TILE], F32)) for k in range(2)]
        ps_g = [ctx.enter_context(nc.psum_tensor(f"ps_g{k}", [128, 2, 512], F32)) for k in range(2)]
        ps_s = ctx.enter_context(nc.psum_tensor("ps_s", [128, 512], F32))
        ps_m = ctx.enter_context(nc.psum_tensor("ps_m", [128, 512], F32))

        z_dram = [nc.dram_tensor(f"z_dram{t}", [N_FEAT, Z_COLS * TILE], F32, kind="Internal") for t in range(CHUNK_TILES)]

        s_zero = sem("s_zero")
        s_const = sem("s_const")
        s_rowno = sem("s_rowno")
        s_pad = sem("s_pad")
        s_raw = [sem(f"s_raw{k}") for k in range(N_ON_CHIP)]
        s_hi = sem("s_hi")
        s_lo = sem("s_lo")
        s_w = sem("s_w")
        s_idx = [sem(f"s_idx{p}") for p in range(2)]
        s_ids = [sem(f"s_ids{p}") for p in range(2)]
        s_ids_first = sem("s_ids_first")
        s_x = [sem(f"s_x{t}") for t in range(CHUNK_TILES)]
        s_place = sem("s_place")
        s_rows = [[sem(f"s_rows{t}_{g}") for g in range(max(N_TGRP))] for t in range(CHUNK_TILES)]
        s_tr = sem("s_tr")
        s_tcopy = [sem(f"s_tcopy{k}") for k in range(2)]
        s_oh = sem("s_oh")
        s_sel = sem("s_sel")
        s_scopy = sem("s_scopy")
        s_place_sel = sem("s_place_sel")
        s_gram = sem("s_gram")
        s_gcopy = [sem(f"s_gcopy{k}") for k in range(2)]
        s_zw = [sem(f"s_zw{t}") for t in range(CHUNK_TILES)]
        s_zr = [sem(f"s_zr{t}") for t in range(CHUNK_TILES)]
        s_mlp = sem("s_mlp")
        s_mcopy = sem("s_mcopy")
        s_y = sem("s_y")

        block = ctx.enter_context(nc.Block())

        def chunks(eng, body):
            body(FIRST)
            with eng.Fori(0, (N_CHUNKS - 2) // 2) as i:
                first = Chunk(i * 2 + 1, i, 1, 1)
                body(first)
                body(first.next())
            body(Chunk(N_CHUNKS - 1, (N_CHUNKS - 1) // 2, (N_CHUNKS - 1) % 2, N_CHUNKS - 1))

        def period(ch, t):
            last = ch.least == N_CHUNKS - 1
            steps = {
                "place": [] if last and t == 1 else [0],
                "tr": [] if last and t == 1 else list(range(N_TGRP[next_tile(ch, t)[0].par])),
                "sel": [] if last else list(range(SEL_CUT)) if t == 0 else list(range(SEL_CUT, ch.next().n_sel())),
                "mlp": [] if ch.least == 0 or last and t == 1 else list(range(LAST_MLP_CUT)) if last else
                       list(range(MLP_CUT)) if t == 0 else list(range(MLP_CUT, MLP_STEPS)),
                "dots": list(range(N_GGRP)),
            }
            order = (LAST_PATTERN if last else PATTERN)[t]
            return [(kind, steps[kind].pop(0)) for kind in order if steps[kind]] + \
                [(kind, n) for kind, left in steps.items() for n in left]

        def cut_now(ch, n):
            return [k for k in range(N_SEL, N_ON_CHIP) if ch.least == 0 and n == 2 * (k - N_SEL) + 1]

        def opening():
            steps = [("sel", 0), ("sel", 1)]
            for n in range(max(N_SEL - 2, N_TGRP[0])):
                steps += [("tr", n)] * (n < N_TGRP[0]) + [("sel", n + 2)] * (n + 2 < N_SEL)
            return steps + [("place", 0)]

        def closing():
            left = [(r, N_CHUNKS - 2, range(CHUNK_TILES)) for r in range(LAST_MLP_CUT, MLP_STEPS)]
            own = [[(r, N_CHUNKS - 1, [t]) for r in range(MLP_STEPS)] for t in range(CHUNK_TILES)]
            order = left[:-1] + own[0][:M1] + left[-1:] + own[0][M1:-1] + own[1][:1] + own[0][-1:] + own[1][1:]
            return [(*step, MLP_STEPS * (N_CHUNKS - 2) + LAST_MLP_CUT + n, LAST_MLP_CUT + n + 1,
                     step[0] in (M1, M1 + M2) and (n == 0 or order[n - 1][1:] == step[1:]))
                    for n, step in enumerate(order)]

        def late(ch, r):
            return r + 1 if ch.least == N_CHUNKS - 1 else 0

        def next_tile(ch, t):
            return (ch, 1) if t == 0 else (ch.next(), 0)

        def copier(ch, t, g):
            return (t * N_TGRP[ch.par] + g) % 2

        def bank_use(ch, t, g, k):
            return ch.half * sum(N_TGRP) + (ch.par * N_TGRP[0] + (t * N_TGRP[ch.par] + g + 1 - k) // 2)

        def table_of(k):
            return tables[(SELECTED + SHARED)[k]].rearrange("(p a) d -> p (a d)", a=SPLIT)

        def onehot_of(k):
            return onehot[2 if N_SHARED % 2 and k == N_ON_CHIP - 1 else k % 2]

        def place_of(k):
            return (k + N_SHARED) % N_ON_CHIP

        def grams(ch, t, u):
            return (ch.c * CHUNK_TILES + t) * N_GGRP + u

        @block.sync
        def _(sp):
            def load_idx(first_tile, par):
                sp.dma_start(idx[par][:, :, :], ids_gath[bass.ds(first_tile, CHUNK_TILES), :, :]
                             .rearrange("t p f -> p t f")).then_inc(s_idx[par], 16)

            def load_ids(sample, par):
                sp.dma_start(ids_row[par][:, :, :],
                             ids_sel[:, bass.ds(sample, CHUNK)].partition_broadcast(128)).then_inc(s_ids[par], 16)

            def load_x(sample, t):
                sp.dma_start(rows[t][:, DENSE_AT, :], x[bass.ds(sample, TILE), :]).then_inc(s_x[t], 16)

            sp.sem_inc(s_y, 16)
            load_idx(0, 0)
            sp.dma_start(ids_row[0][:, 0:OH_AHEAD, :], ids_sel[0:OH_AHEAD, 0:CHUNK].partition_broadcast(128))\
              .then_inc(s_ids_first, 16)
            sp.dma_start(ids_row[0][:, OH_AHEAD:, :], ids_sel[OH_AHEAD:, 0:CHUNK].partition_broadcast(128))\
              .then_inc(s_ids[0], 16)
            load_idx(CHUNK_TILES, 1)
            for t in range(CHUNK_TILES):
                load_x(t * TILE, t)
            for k in range(RAW_BUFS, N_SEL):
                sp.wait_ge(s_lo, k - RAW_BUFS + 1)
                sp.dma_start(table_raw[k], table_of(k)).then_inc(s_raw[k], 16)
            load_ids(CHUNK, 1)
            for dst, src in ((w1p_sb[:, :, :], w1_pairs.rearrange("(k p) n -> p k n", p=PAIR_K)),
                             (w1d_sb[:, :], w1_dense), (w2_sb[:, :, :], w2.rearrange("(k p) n -> p k n", p=128)),
                             (w3_sb[:, :], w3), (b1_sb[:, :], b1), (b2_sb[:, :], b2)):
                sp.dma_start(dst, src).then_inc(s_w, 16)
            for k in range(N_SEL, N_ON_CHIP):
                if k > N_SEL:
                    sp.wait_ge(s_lo, k)
                sp.dma_start(table_raw[k], table_of(k)).then_inc(s_raw[k], 16)

            def bounce(ch, t, copied, read, written, layer_done):
                sp.wait_ge(s_gcopy[0], copied)
                sp.wait_ge(s_gcopy[1], copied)
                if ch.least >= 1:
                    sp.wait_ge(s_zr[t], read)
                q = 32 * t
                sp.dma_start(z_dram[t][:, 0:N_FEAT * TILE], zsb[q:q + N_FEAT, :]).then_inc(s_zw[t], 16)
                sp.dma_start(z_dram[t][:, N_FEAT * TILE:Z_COLS * TILE], zsb[q:q + N_FEAT, 0:HALF_FEAT * TILE])\
                  .then_inc(s_zw[t], 16)
                sp.wait_ge(s_zw[t], written)
                if ch.least >= 1:
                    sp.wait_ge(s_mlp, layer_done)
                base = z_dram[t][:, :]
                for k in range(PAIR_TILES):
                    f0 = k * F_PER_TILE
                    diagonal = bass.AP(tensor=base.tensor, offset=(f0 * Z_COLS + f0 + 1) * TILE,
                                       ap=[[(Z_COLS + 1) * TILE, F_PER_TILE], [TILE, HALF_FEAT], [1, TILE]])
                    sp.dma_start(zpair[ch.par][0:PAIR_K, k, t * TILE:(t + 1) * TILE], diagonal)\
                      .then_inc(s_zr[t], 16)

            def store_y(copied, sample):
                sp.wait_ge(s_mcopy, copied)
                sp.dma_start(out[bass.ds(sample, CHUNK), :].rearrange("n o -> o n"), y_sb[:, :]).then_inc(s_y, 16)

            def held(value):
                if isinstance(value, int):
                    return value
                reg = sp.alloc_register(f"held{len(held_regs)}")
                held_regs.append(reg)
                sp.reg_mov(reg, value)
                return sp.snap(reg)

            held_regs = []

            def body(ch):
                not_last = ch.least < N_CHUNKS - 1
                if not_last:
                    x0, x1 = (ch.c + 1) * CHUNK, (ch.c + 1) * CHUNK + TILE
                    far_sample, far_tile = (ch.c + 2) % N_CHUNKS * CHUNK, (ch.c + 2) % N_CHUNKS * CHUNK_TILES
                if ch.least >= 1:
                    y0 = (ch.c - 1) * CHUNK
                ids_used = held(ch.next().sels())
                transposed = [held(ch.tgroups(t + 1)) for t in range(CHUNK_TILES)]
                y_copied = held(1 + MLP_STEPS * ch.c + (M1 if ch.least == N_CHUNKS - 1 else 0))
                counts = [held(16 * PAIR_TILES * ch.c), held(32 * (ch.c + 1)), held(1 + MLP_STEPS * (ch.c - 1))]
                copied = [held((ch.c * CHUNK_TILES + t + 1) * (N_GGRP // 2)) for t in range(CHUNK_TILES)]
                if not_last:
                    sp.wait_ge(s_oh, ids_used)
                    load_ids(far_sample, ch.par)
                    sp.wait_ge(s_tr, transposed[0])
                    load_x(x0, 0)
                bounce(ch, 0, copied[0], *counts)
                if not_last:
                    sp.wait_ge(s_tr, transposed[1])
                    load_x(x1, 1)
                    load_idx(far_tile, ch.par)
                bounce(ch, 1, copied[1], *counts)
                if ch.least >= 1:
                    store_y(y_copied, y0)

            chunks(sp, body)
            store_y(1 + MLP_STEPS * (N_CHUNKS + 1), BATCH - CHUNK)
            sp.wait_ge(s_y, 16 * (1 + N_CHUNKS))
            for p in range(2):
                sp.wait_ge(s_idx[p], 16 * (1 + (N_CHUNKS - p) // 2))
                sp.wait_ge(s_ids[p], 16 * (1 + (N_CHUNKS - p) // 2))

        @block.gpsimd
        def _(pool):
            pool.iota(row_no_i[:, :], pattern=[[1, SPLIT]], base=0, channel_multiplier=SPLIT).then_inc(s_const, 1)
            pool.memset(ident[:, :], 0.0).then_inc(s_zero, 1)
            pool.wait_ge(s_zero, 1)
            pool.affine_select(out=ident[:, :], in_=ident[:, :], compare_op=ALU.not_equal, fill=1.0,
                               base=0, pattern=[[-1, 128]], channel_multiplier=1).then_inc(s_const, 1)

            def body(ch):
                pool.wait_ge(s_idx[ch.par], 16 * (ch.half + 1))
                for t in range(CHUNK_TILES):
                    for g, feats in enumerate(T_GROUPS[ch.par]):
                        if ch.least >= 1:
                            before = N_TGRP[1 - ch.par]
                            pool.wait_ge(s_tr, ch.tgroups() - (CHUNK_TILES - t) * before + min(g, before - 1) + 1)
                            pool.sem_inc(s_place, 1)
                        for f in feats:
                            if f != DENSE_AT:
                                n = f - (f > DENSE_AT)
                                pool.indirect_dma_start(
                                    rows[t][:, f, :], None, tables[(GATHERED + SHARED)[n]][:, :],
                                    bass.IndirectOffsetOnAxis(ap=idx[ch.par][:, t, n:n + 1].bitcast(U32), axis=0),
                                ).then_inc(s_rows[t][g], 16)

            chunks(pool, body)

        @block.tensor
        def _(pe):
            def transposes(ch, t, g):
                feats = T_GROUPS[ch.par][g]
                always = len([f for f in feats if f < DENSE_AT])
                even = len([f for f in T_GROUPS[0][g] if f > DENSE_AT])
                pe.wait_ge(s_rows[t][g], (ch.c + 1) * (16 * always) + (ch.half + 1) * (16 * even))
                if DENSE_AT in feats:
                    pe.wait_ge(s_x[t], 16 * (ch.c + 1))
                k = copier(ch, t, g)
                if ch.least >= 1 or t * N_TGRP[0] + g >= 2:
                    pe.wait_ge(s_tcopy[k], bank_use(ch, t, g, k))
                for j, f in enumerate(feats):
                    mm = pe.transpose(ps_t[k][:, j, :], rows[t][:, f, :], ident[:, :])
                mm.then_inc(s_tr, 1)

            def select(nxt, k):
                n = nxt.sels() + k
                pe.wait_ge(s_oh, n + 1)
                if nxt.least >= 1 or k >= 1:
                    pe.wait_ge(s_scopy, n)
                if nxt.least == 0 or nxt.least == 1 and k >= N_SEL:
                    pe.wait_ge(s_hi, k + 1)
                    pe.wait_ge(s_lo, k + 1)
                slot = onehot_of(k)
                for a in range(SPLIT):
                    for part in (table_hi, table_lo):
                        mm = pe.matmul(ps_s[:, 0:CHUNK], part[k][:, a * DIM:(a + 1) * DIM], slot[0:SEL_K, a, :],
                                       start=(a == 0 and part is table_hi),
                                       stop=(a == SPLIT - 1 and part is table_lo))
                mm.then_inc(s_sel, 1)

            def mlp(done, par, r, tiles, filled, late, input_last):
                if late <= 1:
                    pe.wait_ge(s_mcopy, 1 + done)
                else:
                    pe.wait_ge(s_mcopy, done)

                def wait_last_input():
                    if late > 1 and input_last:
                        pe.wait_ge(s_mcopy, 1 + done)

                bank = ps_s if late and late % 2 == 0 else ps_m
                if r == 0:
                    for t in tiles:
                        pe.wait_ge(s_zr[t], 16 * PAIR_TILES * filled)
                cols = slice(tiles[0] * TILE, (tiles[-1] + 1) * TILE)
                o = bank[:, cols]
                if r < M1:
                    w = slice(r * 128, (r + 1) * 128)
                    pe.matmul(o, w1d_sb[:, w], denseT[par][:, cols], start=True, stop=False)
                    for k in range(PAIR_TILES):
                        mm = pe.matmul(o, w1p_sb[:, k, w], zpair[par][0:PAIR_K, k, cols],
                                       start=False, stop=(k == PAIR_TILES - 1))
                elif r < M1 + M2:
                    m = r - M1
                    for k in range(M1):
                        if k == M1 - 1:
                            wait_last_input()
                        mm = pe.matmul(o, w2_sb[:, k, m * 128:(m + 1) * 128], h1[:, k, cols],
                                       start=(k == 0), stop=(k == M1 - 1))
                else:
                    for k in range(M2):
                        if k == M2 - 1:
                            wait_last_input()
                        mm = pe.matmul(bank[0:1, cols], w3_sb[:, k:k + 1], h2[:, k, cols],
                                       start=(k == 0), stop=(k == M2 - 1))
                mm.then_inc(s_mlp, 1)

            def dots(ch, t, u):
                if u == 0:
                    for k in range(2):
                        pe.wait_ge(s_tcopy[k], bank_use(ch, t + 1, 0, k))
                    pe.wait_ge(s_place_sel, ch.c * CHUNK_TILES + t + 1)
                if ch.least >= 1 or t >= 1 or u >= 2:
                    pe.wait_ge(s_gcopy[u % 2], (ch.c * CHUNK_TILES + t) * (N_GGRP // 2) + u // 2)
                for n in range(GRAM_SAMPLES // QUAD):
                    b = u * GRAM_SAMPLES + n * QUAD
                    mm = pe.matmul(ps_g[u % 2][0:GRAM_M, n // 4, (n % 4) * GRAM_N:(n % 4 + 1) * GRAM_N],
                                   xT[t].rearrange("p b f -> p (b f)")[:, b * FEAT_PAD:b * FEAT_PAD + GRAM_M],
                                   xT[t][:, b:b + QUAD, 0:N_FEAT], start=True, stop=True)
                mm.then_inc(s_gram, 1)

            def body(ch):
                for t in range(CHUNK_TILES):
                    for kind, n in period(ch, t):
                        if kind == "tr":
                            transposes(*next_tile(ch, t), n)
                        elif kind == "sel":
                            select(ch.next(), n)
                        elif kind == "mlp":
                            mlp(MLP_STEPS * (ch.c - 1) + n, 1 - ch.par, n, range(CHUNK_TILES), ch.c, late(ch, n),
                                n in (M1, M1 + M2))
                        elif kind == "dots":
                            dots(ch, t, n)

            pe.sem_inc(s_mlp, 1)
            pe.wait_ge(s_pad, 1)
            pe.wait_ge(s_const, 2)
            for kind, n in opening():
                if kind == "tr":
                    transposes(FIRST, 0, n)
                elif kind == "sel":
                    select(FIRST, n)
            pe.wait_ge(s_w, 16 * 6)
            pe.wait_ge(s_lo, N_SEL)
            chunks(pe, body)
            for r, c, tiles, done, number, input_last in closing():
                mlp(done, c % 2, r, tiles, c + 1, number, input_last)

        def copy_transposes(copy, eng, ch, t, g, mine):
            feats = T_GROUPS[ch.par][g]
            eng.wait_ge(s_tr, ch.tgroups(t, g) + 1)
            last = copy(xT[t].rearrange("p b f -> p f b")[:, feats[0]:feats[-1] + 1, :], ps_t[mine][:, 0:len(feats), :])
            if DENSE_AT in feats:
                last = copy(denseT[ch.par][:, t * TILE:(t + 1) * TILE], ps_t[mine][:, DENSE_AT - feats[0], :])
            last.then_inc(s_tcopy[mine], 1)

        def copy_dots(copy, eng, ch, t, u, mine):
            q = 32 * t
            if ch.least >= 1 and u < 2:
                eng.wait_ge(s_zw[t], 32 * ch.c)
            eng.wait_ge(s_gram, grams(ch, t, u) + 1)
            dst = zsb[q:q + N_FEAT, :].rearrange("p (g u h n j) -> p u j h n g", u=N_GGRP, h=2, n=4, j=QUAD)
            for j in range(QUAD):
                src = ps_g[mine][32 * j:32 * j + N_FEAT, :, 0:4 * GRAM_N]\
                    .rearrange("p h (n c) -> p h n c", c=GRAM_N)[:, :, :, j * N_FEAT:(j + 1) * N_FEAT]
                last = copy(dst[:, u, j, :, :, :], src)
            last.then_inc(s_gcopy[mine], 1)

        @block.scalar
        def _(act):
            def copy(dst, src):
                return act.activation(dst, src, ACT.Copy)

            def copy_selected(nxt, k):
                act.wait_ge(s_sel, nxt.sels() + k + 1)
                copy(picked[nxt.par][:, place_of(k), :], ps_s[:, 0:CHUNK]).then_inc(s_scopy, 1)

            def copy_mlp(done, r, tiles, c, late):
                act.wait_ge(s_mlp, 1 + done + 1)
                bank = ps_s if late and late % 2 == 0 else ps_m
                cols = slice(tiles[0] * TILE, (tiles[-1] + 1) * TILE)
                if r < M1:
                    last = act.activation(h1[:, r, cols], bank[:, cols], ACT.Relu, bias=b1_sb[:, r:r + 1])
                elif r < M1 + M2:
                    m = r - M1
                    last = act.activation(h2[:, m, cols], bank[:, cols], ACT.Relu, bias=b2_sb[:, m:m + 1])
                else:
                    act.wait_ge(s_y, 16 * (1 + c))
                    last = copy(y_sb[:, cols], bank[0:1, cols])
                last.then_inc(s_mcopy, 1)

            def body(ch):
                for t in range(CHUNK_TILES):
                    for kind, n in period(ch, t):
                        if kind == "tr":
                            nxt, nt = next_tile(ch, t)
                            if copier(nxt, nt, n) == 0:
                                copy_transposes(copy, act, nxt, nt, n, 0)
                        elif kind == "sel":
                            for k in cut_now(ch, n):
                                upper_part(k)
                            copy_selected(ch.next(), n)
                        elif kind == "mlp":
                            copy_mlp(MLP_STEPS * (ch.c - 1) + n, n, range(CHUNK_TILES), ch.c - 1, late(ch, n))
                        elif kind == "dots" and n % 2 == 0:
                            copy_dots(copy, act, ch, t, n, 0)

            def upper_part(k):
                act.wait_ge(s_raw[k], 16)
                copy(table_hi[k][:, :], table_raw[k]).then_inc(s_hi, 1)

            act.sem_inc(s_mcopy, 1)
            for k in range(RAW_BUFS):
                act.dma_start(table_raw[k], table_of(k)).then_inc(s_raw[k], 16)
            for k in range(2):
                upper_part(k)
            for kind, n in opening():
                if kind == "tr":
                    copy_transposes(copy, act, FIRST, 0, n, copier(FIRST, 0, n))
                elif kind == "sel":
                    if n + 2 < N_SEL:
                        upper_part(n + 2)
                    copy_selected(FIRST, n)
            act.wait_ge(s_w, 16 * 6)
            chunks(act, body)
            for r, c, tiles, done, number, _ in closing():
                copy_mlp(done, r, tiles, c, number)

        @block.vector
        def _(dve):
            def copy(dst, src):
                return dve.tensor_copy(dst, src)

            def lower_part(k):
                dve.wait_ge(s_hi, k + 1)
                dve.tensor_tensor(table_lo[k][:, :], table_raw[k], table_hi[k][:, :].bitcast(F32),
                                  ALU.subtract).then_inc(s_lo, 1)

            def make_onehot(ch, k):
                n = ch.sels() + k
                if ch.least >= 1 or k >= OH_AHEAD:
                    dve.wait_ge(s_sel, n - OH_AHEAD + 1)
                if ch.least == 0 and k == 0:
                    dve.wait_ge(s_ids_first, 16)
                elif k == (OH_AHEAD if ch.least == 0 else 0):
                    dve.wait_ge(s_ids[ch.par], 16 * (ch.half + 1))
                slot = onehot_of(k)
                for a in range(SPLIT):
                    last = dve.tensor_scalar(slot[0:SEL_K, a, :], ids_row[ch.par][0:SEL_K, k, :],
                                             row_no[0:SEL_K, a:a + 1], None, ALU.is_equal)
                last.then_inc(s_oh, 1)

            def ahead(nxt, k):
                if k + OH_AHEAD < nxt.n_sel():
                    make_onehot(nxt, k + OH_AHEAD)
                else:
                    make_onehot(nxt.next(), k + OH_AHEAD - nxt.n_sel())

            def place_selected(ch, t):
                dve.wait_ge(s_scopy, ch.next().sels())
                if ch.least >= 1:
                    dve.wait_ge(s_gram, grams(ch, t, 0) - CHUNK_TILES * N_GGRP + N_GGRP)
                first = 0 if ch.par else N_SHARED
                dve.tensor_copy(xT[t].rearrange("p b f -> p f b")[:, DENSE_AT + 1 + first:N_FEAT, :],
                                picked[ch.par][:, first:, t * TILE:(t + 1) * TILE]).then_inc(s_place_sel, 1)

            def body(ch):
                for t in range(CHUNK_TILES):
                    nxt, nt = next_tile(ch, t)
                    for kind, n in period(ch, t):
                        if kind == "place":
                            place_selected(nxt, nt)
                        elif kind == "tr" and copier(nxt, nt, n) == 1:
                            copy_transposes(copy, dve, nxt, nt, n, 1)
                        elif kind == "sel":
                            for k in cut_now(ch, n):
                                lower_part(k)
                            ahead(ch.next(), n)
                        elif kind == "dots" and n % 2 == 1:
                            copy_dots(copy, dve, ch, t, n, 1)

            for t in range(CHUNK_TILES):
                last = dve.memset(xT[t][:, :, N_FEAT:FEAT_PAD], 0.0)
            last.then_inc(s_pad, 1)
            dve.wait_ge(s_const, 1)
            dve.tensor_copy(row_no[:, :], row_no_i[:, :]).then_inc(s_rowno, 1)
            dve.wait_ge(s_rowno, 1)
            for k in range(OH_AHEAD):
                make_onehot(FIRST, k)
                lower_part(k)
            for kind, n in opening():
                if kind == "sel":
                    ahead(FIRST, n)
                    if n + 2 < N_SEL:
                        lower_part(n + 2)
                elif kind == "place":
                    place_selected(FIRST, 0)
            chunks(dve, body)


def pair_rows():
    first, second = np.triu_indices(N_FEAT, k=1)
    row_of = {(int(a), int(b)): r for r, (a, b) in enumerate(zip(first, second))}
    rows = []
    for f in range(N_FEAT):
        for k in range(1, HALF_FEAT + 1):
            a, b = ORDER[f], ORDER[(f + k) % N_FEAT]
            rows.append(row_of[min(a, b), max(a, b)])
    return np.array(rows)


def kernel(**inputs):
    from concourse import bacc
    from concourse.bass_utils import run_bass_kernel_spmd

    a = {k: np.asarray(v) for k, v in inputs.items()}
    lay = np.ascontiguousarray
    arrays = {
        "ids_gath": lay(a["ids"][:, GATHERED + SHARED].reshape(BATCH // TILE, TILE, N_GATH + N_SHARED)),
        "ids_sel": lay(a["ids"][:, SELECTED + SHARED].T),
        "x": lay(a["r_dense_x"]),
        **{f"tbl_{t}": lay(a[f"tbl_{t}"]) for t in range(N_TABLES)},
        "w1_pairs": lay(a["W_top1"][pair_rows()]),
        "w1_dense": lay(a["W_top1"][N_PAIRS:]),
        "b1": lay(a["b_top1"].reshape(M1, 128).T),
        "w2": lay(a["W_top2"]),
        "b2": lay(a["b_top2"].reshape(M2, 128).T),
        "w3": lay(a["W_top3"].reshape(M2, 128).T),
    }
    nc = bacc.Bacc("TRN2", target_bir_lowering=False, num_devices=1)
    arrays = {f"in_{n}": v for n, v in arrays.items()}
    dram = {n: nc.dram_tensor(n, v.shape, mybir.dt.from_np(v.dtype), kind="ExternalInput").ap() for n, v in arrays.items()}
    out = nc.dram_tensor("out_y", (BATCH, 1), F32, kind="ExternalOutput").ap()
    d = lambda n: dram[f"in_{n}"]
    build(nc, d("ids_gath"), d("ids_sel"), d("x"), [d(f"tbl_{t}") for t in range(N_TABLES)],
          d("w1_pairs"), d("w1_dense"), d("b1"), d("w2"), d("b2"), d("w3"), out)
    r = run_bass_kernel_spmd(nc, [arrays], core_ids=[0])
    return r.results[0]["out_y"]
```
